# Optimizing a Trainium2 kernel written in Bass

```python
import numpy as np
import jax
import jax.numpy as jnp

def _softmax(x, axis=-1):
    return jax.nn.softmax(x, axis=axis)
def _gelu(x):
    return jax.nn.gelu(x, approximate=True)
def _silu(x):
    return jax.nn.silu(x)
def _sigmoid(x):
    return jax.nn.sigmoid(x)
def _layernorm(x, axis=-1, eps=1e-5):
    m = jnp.mean(x, axis=axis, keepdims=True)
    v = jnp.var(x, axis=axis, keepdims=True)
    return (x - m) / jnp.sqrt(v + eps)
def _scatter_add(tgt, idx, src, axis=0):
    return tgt.at[idx].add(src)
def _segment_sum(src, seg, n):
    return jax.ops.segment_sum(src, seg, n)

kernel_name = 'mk_adj_preln_d1_adj_256_cdfd18'

def setup_inputs(seed: int = 0):
    np.random.seed(seed)
    _w = jnp.asarray
    def _rec_inputs():
        import jax
        import jax.numpy as jnp
        _gk = jax.random.key(seed)
        x = -0.0005207 + 1.001 * jax.random.normal(jax.random.fold_in(_gk, 1), (8, 2048, 256), jnp.float32)
        _a = jax.random.bernoulli(jax.random.fold_in(_gk, 2), 0.00390625, (8, 2048, 2048))
        adj = _a.astype(jnp.int32)
        return x, adj
    x, adj = _rec_inputs()
    def _L0_gnn_setup():
        import jax, jax.numpy as jnp
        import numpy as np
        DIM = 256
        HEADS = 8
        HEAD_DIM = DIM // HEADS
        DFF = 4 * DIM
        EPS = 1e-05

        def _layernorm(x, g, b):
            m = jnp.mean(x, axis=-1, keepdims=True)
            v = jnp.mean(jnp.square(x - m), axis=-1, keepdims=True)
            return (x - m) * jax.lax.rsqrt(v + EPS) * g + b
        key = jax.random.key(seed)
        ks = jax.random.split(key, 12)
        B, N = (8, 1024)
        s = 1.0 / np.sqrt(DIM)
        x = jax.random.normal(ks[0], (B, N, DIM), dtype=jnp.float32)
        adj = jax.random.randint(ks[1], (B, N, N), 0, 2, dtype=jnp.int32)
        return {'x': x, 'adj': adj, 'Wqkv': jax.random.normal(ks[2], (3 * DIM, DIM), jnp.float32) * s, 'bqkv': jnp.zeros((3 * DIM,), jnp.float32), 'Wo': jax.random.normal(ks[3], (DIM, DIM), jnp.float32) * s, 'bo': jnp.zeros((DIM,), jnp.float32), 'ln1_g': jnp.ones((DIM,), jnp.float32), 'ln1_b': jnp.zeros((DIM,), jnp.float32), 'W1': jax.random.normal(ks[4], (DFF, DIM), jnp.float32) * s, 'b1': jnp.zeros((DFF,), jnp.float32), 'W2': jax.random.normal(ks[5], (DIM, DFF), jnp.float32) * (1.0 / np.sqrt(DFF)), 'b2': jnp.zeros((DIM,), jnp.float32), 'ln2_g': jnp.ones((DIM,), jnp.float32), 'ln2_b': jnp.zeros((DIM,), jnp.float32)}
    _L0_gnn_all = _L0_gnn_setup()
    _L0_gnn_in = {k: v for k, v in _L0_gnn_all.items() if k in ('Wqkv', 'bqkv', 'Wo', 'bo', 'ln1_g', 'ln1_b', 'W1', 'b1', 'W2', 'b2', 'ln2_g', 'ln2_b', )}
    del _L0_gnn_all

    return {
        "x": x,
        "adj": adj,
        "L0_gnn_Wqkv": _L0_gnn_in["Wqkv"],
        "L0_gnn_bqkv": _L0_gnn_in["bqkv"],
        "L0_gnn_Wo": _L0_gnn_in["Wo"],
        "L0_gnn_bo": _L0_gnn_in["bo"],
        "L0_gnn_ln1_g": _L0_gnn_in["ln1_g"],
        "L0_gnn_ln1_b": _L0_gnn_in["ln1_b"],
        "L0_gnn_W1": _L0_gnn_in["W1"],
        "L0_gnn_b1": _L0_gnn_in["b1"],
        "L0_gnn_W2": _L0_gnn_in["W2"],
        "L0_gnn_b2": _L0_gnn_in["b2"],
        "L0_gnn_ln2_g": _L0_gnn_in["ln2_g"],
        "L0_gnn_ln2_b": _L0_gnn_in["ln2_b"],
    }

def reference(x, adj, L0_gnn_Wqkv, L0_gnn_bqkv, L0_gnn_Wo, L0_gnn_bo, L0_gnn_ln1_g, L0_gnn_ln1_b, L0_gnn_W1, L0_gnn_b1, L0_gnn_W2, L0_gnn_b2, L0_gnn_ln2_g, L0_gnn_ln2_b):
    import jax
    import jax.numpy as jnp
    def _L0_gnn_ref(x, adj, Wqkv, bqkv, Wo, bo, ln1_g, ln1_b, W1, b1, W2, b2, ln2_g, ln2_b):
        import jax, jax.numpy as jnp
        import numpy as np
        DIM = 256
        HEADS = 8
        HEAD_DIM = DIM // HEADS
        DFF = 4 * DIM
        EPS = 1e-05

        def _layernorm(x, g, b):
            m = jnp.mean(x, axis=-1, keepdims=True)
            v = jnp.mean(jnp.square(x - m), axis=-1, keepdims=True)
            return (x - m) * jax.lax.rsqrt(v + EPS) * g + b
        B, N, _ = x.shape
        eye = jnp.eye(N, dtype=bool)[None]
        allowed = (adj > 0) | (jnp.swapaxes(adj, 1, 2) > 0) | eye
        qkv = x @ Wqkv.T + bqkv
        q, k, v = jnp.split(qkv, 3, axis=-1)

        def heads(t):
            return t.reshape(B, N, HEADS, HEAD_DIM).transpose(0, 2, 1, 3)
        q, k, v = (heads(q), heads(k), heads(v))
        scale = 1.0 / np.sqrt(HEAD_DIM)
        scores = jnp.einsum('bhqd,bhkd->bhqk', q * scale, k)
        scores = jnp.where(allowed[:, None], scores, -jnp.inf)
        attn = jax.nn.softmax(scores, axis=-1)
        ctx = jnp.einsum('bhqk,bhkd->bhqd', attn, v)
        ctx = ctx.transpose(0, 2, 1, 3).reshape(B, N, DIM)
        attn_out = ctx @ Wo.T + bo
        x = _layernorm(x + attn_out, ln1_g, ln1_b)
        ff = jax.nn.relu(x @ W1.T + b1) @ W2.T + b2
        x = _layernorm(x + ff, ln2_g, ln2_b)
        return x

    h = jnp.maximum(_layernorm(x, axis=-1), 0.0)
    x = x + _L0_gnn_ref(h, adj, L0_gnn_Wqkv, L0_gnn_bqkv, L0_gnn_Wo, L0_gnn_bo, L0_gnn_ln1_g, L0_gnn_ln1_b, L0_gnn_W1, L0_gnn_b1, L0_gnn_W2, L0_gnn_b2, L0_gnn_ln2_g, L0_gnn_ln2_b)
    return x


_drawn_inputs = setup_inputs


def setup_inputs(seed=0):
    import zlib

    import numpy as np

    out = dict(_drawn_inputs(seed))
    spreads = {'L0_gnn_bqkv': (0.0, 0.1),
     'L0_gnn_bo': (0.0, 0.1),
     'L0_gnn_ln1_g': (1.0, 0.2),
     'L0_gnn_ln1_b': (0.0, 0.1),
     'L0_gnn_b1': (0.0, 0.1),
     'L0_gnn_b2': (0.0, 0.1),
     'L0_gnn_ln2_g': (1.0, 0.2),
     'L0_gnn_ln2_b': (0.0, 0.1)}
    factors = {}
    for name, (base, spread) in spreads.items():
        noise = np.random.default_rng([zlib.crc32(name.encode()), seed]).standard_normal(out[name].shape)
        drawn = base * np.exp(spread * noise) if base else spread * noise
        out[name] = jnp.asarray(drawn.astype(out[name].dtype))
    for name, factor in factors.items():
        out[name] = (out[name] * factor).astype(out[name].dtype)
    return out
```

```python
from contextlib import ExitStack

import numpy as np

import concourse.bass as bass
from concourse import mybir

F32 = mybir.dt.float32
F16 = mybir.dt.float16
BF16 = mybir.dt.bfloat16
I32 = mybir.dt.int32
U8 = mybir.dt.uint8
ALU = mybir.AluOpType
ACT = mybir.ActivationFunctionType
AX = mybir.AxisListType
RMAX = bass.bass_isa.ReduceOp.max

P = 128
D = 256
H = 8
DH = D // H
HG = P // DH
G = H // HG
F = 4 * D
FC = F // P
KD = D // P
T = 512
TJ = T // P
EPS = 1e-5
QK_SCALE = 64.0
SAFE_SCORE = 58.0
EXP_SCALE = 1.0 / (QK_SCALE * QK_SCALE * float(np.sqrt(DH)))
SAFE_PRODUCT = (SAFE_SCORE / EXP_SCALE) ** 2
SAFE_NORM = 6e4 ** 2
RING = 3
PR = 4
LAG = 2

POST_PE = {"A": 1, "B": 10, "C0": 12, "C1": 14, "C2": 16, "C3": 19, "D0": 22, "D1": 23, "D2": 24, "D3": 25}
MASK_PE = {"M0": 4, "M1": 8, "M2": 17, "M3": 27}
POST_ACT = {"B": 10, "C0": 12, "C1": 14, "C2": 16, "C3": 19}
MASK_ACT = {"S0": 2, "S1": 6, "S2": 13, "S3": 21}
POST_DVE = {"A": 1, "N1": 3, "D0": 22, "D1": 23, "D2": 24, "D3": 25, "N2": 27, "OUT": 31}
MASK_DVE = {"M0": 4, "M1": 8, "M2": 17, "M3": 27, "EYE": 29}
POST_POOL = {"R1": 2, "G1": 4, "B1": 6, "X1": 8, "R2": 26, "G2": 28, "B2": 29}
RING_TAGS = ("A", "B", "C0", "C1", "C2", "C3", "D0", "D1", "D2", "D3", "M0", "M1", "M2", "M3")
POST_TAGS = RING_TAGS[:10]


def at(step, *tables):
    return [tag for table in tables for tag, s in table.items() if s == step]


class Uses:

    def __init__(self, steps):
        self.steps = steps
        self.start, self.place, n = {}, {}, 0
        self.start["prep"] = 0
        for c in range(TJ):
            for tag in ("T", "Q", "K", "V", "NQ", "NK", "M"):
                self.place["prep", c, tag] = n
                n += 1
        for kind, post, mask in (("first", 0, 1), ("middle", 1, 1), ("last", 1, 0)):
            self.start[kind], m = n, 0
            for i in range(steps):
                for half in range(2):
                    self.place[kind, i, half] = m
                    m += 1
                for tag in at(i, *([POST_PE] if post else []), *([MASK_PE] if mask else [])):
                    self.place[kind, tag] = m
                    m += 1
            n += m * (2 if kind == "middle" else 1)
            if kind == "middle":
                self.middle = m
        self.start["post"] = n
        for m, tag in enumerate(POST_TAGS):
            self.place["post", tag] = m
        self.total = n + len(POST_TAGS)
        assert self.total % RING == 0 and self.middle % RING == 0

    def of(self, kind, *key):
        return self.start[kind] + self.place[(kind, *key)] if kind != "prep" else self.place[(kind, *key)]


def gnn_layer(nc, x, adj, wqkvT, bqkv, woT, bo, g1, b1n, w1T, b1, w2T, b2, g2, b2n, out):
    B, N, _ = x.shape
    KT = N // P
    QT = N // T
    STEPS = G * KT
    PAIRS = STEPS // 2
    assert QT == 4 and QT == TJ
    uses = Uses(STEPS)

    stack = ExitStack()
    with stack:
        def sb(name, shape, dt):
            return stack.enter_context(nc.sbuf_tensor(name, shape, dt))

        def sem(name):
            return stack.enter_context(nc.semaphore(name))

        def scratch(name, shape, dt):
            return nc.dram_tensor(name, shape, dt, kind="Internal").ap()

        h_dram = scratch("h_dram", (B, N, D), F32)
        qk_dram = scratch("qk_dram", (B, 2, 2, D, N), F16)
        qk32_dram = scratch("qk32_dram", (B, 2, D, N), F32)
        v_dram = scratch("v_dram", (B, N, D), F32)
        ctx_dram = scratch("ctx_dram", (D, T), F32)

        wqkv_sb = sb("wqkv_sb", [P, KD, 3 * D], F32)
        wo_sb = sb("wo_sb", [P, KD, D], F32)
        w1_sb = sb("w1_sb", [P, KD, F], F32)
        w2_sb = sb("w2_sb", [P, FC, D], F32)
        rows = sb("rows", [P, 6, D], F32)
        qk_bias = sb("qk_bias", [P, 2 * KD], F32)
        v_bias = sb("v_bias", [P, KD], F32)
        mlp_bias = sb("mlp_bias", [P, FC], F32)
        ones = sb("ones", [P, P], F32)
        ident = sb("ident", [P, P], F32)
        ident16 = sb("ident16", [P, P], BF16)
        head_ones = sb("head_ones", [P, P], BF16)
        minus_half = sb("minus_half", [P, TJ], F32)

        mask = sb("mask", [P, 2 * KT, T], U8)
        k_stack = sb("k_stack", [P, H, N], F16)
        q_stack = sb("q_stack", [P, H, T], F16)
        v_sb = sb("v_sb", [P, KT, D], F32)
        probs = sb("probs", [P, PR, HG, T], F32)
        pairs = sb("pairs", [P, 2, HG, T], F32)
        ctxT = sb("ctxT", [P, G, T], F32)
        rden = sb("rden", [P, T], F32)
        adj_rows = sb("adj_rows", [P, TJ, T], I32)
        adj_cols = sb("adj_cols", [P, TJ, T], I32)
        cols_sign = sb("cols_sign", [P, TJ, T], BF16)
        y = sb("y", [P, TJ, D], F32)
        z = sb("z", [P, TJ, D], F32)
        yT = sb("yT", [P, KD, T], F32)
        x_res = yT[:].rearrange("p k t -> p (k t)").rearrange("p (j d) -> p j d", d=D)
        mlp = sb("mlp", [P, FC, T], F32)
        stats = sb("stats", [P, TJ, 6], F32)
        mean_var = sb("mean_var", [P, TJ, 2], F32)
        var_eps = sb("var_eps", [P, TJ], F32)
        rstd = sb("rstd", [P, TJ], F32)

        pool = probs[:].rearrange("p a h t -> p (a h t)")

        def lent(offset, n, dt=F32):
            return pool[:, offset:offset + n].bitcast(dt) if dt != F32 else pool[:, offset:offset + n]

        W = TJ * D
        h_buf = [lent(i * W, W).rearrange("p (j d) -> p j d", d=D) for i in range(2)]
        hT = lent(2 * W, W).rearrange("p (k t) -> p k t", t=T)
        qk32 = [lent((3 + i) * W, W).rearrange("p (g t) -> p g t", t=T) for i in range(2)]
        high = [lent(5 * W + i * W // 2, W // 2, F16).rearrange("p (g t) -> p g t", t=T) for i in range(2)]
        low = [lent(6 * W + i * W // 2, W // 2, F16).rearrange("p (g t) -> p g t", t=T) for i in range(2)]
        square = [lent(7 * W + i * W // 2, W // 2, BF16).rearrange("p (g t) -> p g t", t=T) for i in range(2)]
        norms_q = sb("norms_q", [P, B, G * TJ], F32)
        norms_k = sb("norms_k", [P, B, G * TJ], F32)
        products = sb("products", [P, B, G * TJ], F32)
        unsafe = sb("unsafe", [P, 4], F32)
        unsafe_int = sb("unsafe_int", [P, 1], I32)

        ring = [stack.enter_context(nc.psum_tensor(f"ring{i}", [P, 2, T], F32)) for i in range(RING)]
        ctx_ps = stack.enter_context(nc.psum_tensor("ctx_ps", [P, T], F32))
        den_ps = stack.enter_context(nc.psum_tensor("den_ps", [P, T], F32))

        filled = sem("filled")
        drained = [sem(f"drained{i}") for i in range(RING)]
        consts_made = sem("consts_made")
        half_made = sem("half_made")
        weights_loaded = sem("weights_loaded")
        bv_spread = sem("bv_spread")
        bo_made = sem("bo_made")
        bias_scaled = sem("bias_scaled")
        setup_full = sem("setup_full")
        x_loaded = [sem(f"x_loaded{i}") for i in range(2)]
        prep_stats = sem("prep_stats")
        prep_meanvar = sem("prep_meanvar")
        prep_veps = sem("prep_veps")
        prep_rstd = sem("prep_rstd")
        prep_normed = sem("prep_normed")
        h_ready = sem("h_ready")
        hres_made = sem("hres_made")
        h_stored = [sem(f"h_stored{i}") for i in range(2)]
        high_ready = sem("high_ready")
        low_ready = sem("low_ready")
        square_ready = sem("square_ready")
        qk_stored = [sem("q_stored"), sem("k_stored")]
        k_loaded = sem("k_loaded")
        v_stored = sem("v_stored")
        rows_loaded = sem("rows_loaded")
        cols_loaded = sem("cols_loaded")
        cols_signed = sem("cols_signed")
        mask_ready = sem("mask_ready")
        q_loaded = [sem(f"q_loaded{g}") for g in range(G)]
        exp_done = sem("exp_done")
        pairs_ready = sem("pairs_ready")
        pv_done = sem("pv_done")
        den_done = sem("den_done")
        rden_ready = sem("rden_ready")
        ctx_ready = sem("ctx_ready")
        y_loaded = sem("y_loaded")
        xres_loaded = sem("xres_loaded")
        y_stats = sem("y_stats")
        y_meanvar = sem("y_meanvar")
        y_veps = sem("y_veps")
        y_rstd = sem("y_rstd")
        y_normed = sem("y_normed")
        y_scaled = sem("y_scaled")
        y_ready = sem("y_ready")
        z_ready = sem("z_ready")
        z_stats = sem("z_stats")
        z_meanvar = sem("z_meanvar")
        z_veps = sem("z_veps")
        z_rstd = sem("z_rstd")
        z_normed = sem("z_normed")
        z_scaled = sem("z_scaled")
        z_shifted = sem("z_shifted")
        out_made = sem("out_made")
        out_stored = sem("out_stored")
        products_made = sem("products_made")
        flag_spread = sem("flag_spread")
        flag_made = sem("flag_made")
        turn = sem("turn")

        passed = sem("passed")

        def wait_apart(eng, semaphore, value):
            eng.wait_ge(semaphore, value)
            eng.sem_inc(passed, 1)

        N_WEIGHTS = 13

        def bank2(slot, n):
            return ring[slot][:].rearrange("p a (c n) -> p (a c) n", n=n)

        class Use:

            def __init__(self, b, kind, *key, m=0):
                u = uses.of(kind, *key)
                self.slot = u % RING
                per = uses.total // RING
                self.before = b * per + m * (uses.middle // RING) + u // RING
                self.count = b * uses.total + m * uses.middle + u + 1
                self.tile = ring[self.slot]

            def wait_filled(self, eng):
                eng.wait_ge(filled, self.count)

            def wait_drained(self, eng):
                eng.wait_ge(drained[self.slot], self.before + 1 + 1)

        PIECE = 35
        MASKED = TJ * PIECE + 1
        PASS1, PASS2 = 5, 10
        MAXIMUM = 51 + KT * PASS1
        SUMS = MAXIMUM + 1
        HEAD = SUMS + KT * PASS2 + 18
        GENERAL = MASKED + H * HEAD + 16
        LOWEST = -3e38
        flat = probs[:].rearrange("p a h t -> p (a h t)")
        gen_q = flat[0:DH, 0:T]
        gen_k = flat[0:DH, T:T + N]
        gen_v = flat[:, T + N:T + N + KT * DH].rearrange("p (k d) -> p k d", d=DH)
        o = T + N + KT * DH
        gen_k_tile, gen_v_tile = flat[0:DH, o:o + P], flat[:, o + P:o + P + DH]
        o += T
        gen_max, gen_s, gen_bias, gen_ctx, gen_den, gen_out = (
            flat[:, o + i * T:o + (i + 1) * T] for i in range(6))
        o += 6 * T
        gen_ctxT = flat[:, o:o + G * T].rearrange("p (g t) -> p g t", t=T)

        class GeneralUse:

            def __init__(self, u, tag):
                i = POST_TAGS.index(tag)
                self.slot = i % RING
                own = len(range(self.slot, len(POST_TAGS), RING))
                self.before = B * (uses.total // RING) + u * own + i // RING
                self.count = B * uses.total + u * len(POST_TAGS) + i + 1
                self.tile = ring[self.slot]

            wait_filled, wait_drained = Use.wait_filled, Use.wait_drained

        def general(eng, unit):
            eng.wait_ge(flag_made, 1)
            flag = eng.value_load(unsafe_int[0:1, 0:1])
            with eng.If(flag > 0):
                with eng.Fori(0, B) as b:
                    with eng.Fori(0, QT) as q:
                        u = b * QT + q
                        unit(b, q, u, u + B * QT)

        def places(eng, b, unit):
            unit(b, 0, "first", 0)
            with eng.Fori(0, QT - 2) as m:
                unit(b, m + 1, "middle", m)
            unit(b, QT - 1, "last", 0)

        block = stack.enter_context(nc.Block())

        @block.sync
        def _(sp):
            for dst, src in (
                (wqkv_sb[:], wqkvT.rearrange("(k p) n -> p k n", p=P)),
                (wo_sb[:], woT.rearrange("(k p) n -> p k n", p=P)),
                (w1_sb[:], w1T.rearrange("(k p) n -> p k n", p=P)),
                (w2_sb[:], w2T.rearrange("(k p) n -> p k n", p=P)),
                (qk_bias[:], bqkv[0:2 * D].rearrange("(c p) -> p c", p=P)),
                (v_bias[:], bqkv[2 * D:3 * D].rearrange("(c p) -> p c", p=P)),
                (mlp_bias[:], b1.rearrange("(c p) -> p c", p=P)),
                *[(rows[:, i, :], v.partition_broadcast(P)) for i, v in enumerate((g1, b1n, g2, b2n, b2, bo))],
            ):
                with nc.allow_non_contiguous_dma(reason="small vectors, once"):
                    sp.dma_start(dst, src).then_inc(weights_loaded, 16)

            def load_x(b, c):
                sp.dma_start(h_buf[c % 2], x[b, c * T:(c + 1) * T, :].rearrange("(j p) d -> p j d", p=P)) \
                    .then_inc(x_loaded[c % 2], 16)

            def load_adj(b, q, piece, before):
                n = b * QT + q
                if piece:
                    before.wait_drained(sp)
                else:
                    sp.wait_ge(mask_ready, n + 1)
                sp.dma_start(adj_rows[:], adj[b, piece * T:(piece + 1) * T, bass.ds(q * T, T)]
                             .rearrange("(j p) t -> p j t", p=P)).then_inc(rows_loaded, 16)
                sp.wait_ge(cols_signed, n * TJ + piece + 1)
                sp.dma_start(adj_cols[:], adj[b, bass.ds(q * T, T), piece * T:(piece + 1) * T]
                             .rearrange("(j p) t -> p j t", p=P)).then_inc(cols_loaded, 16)

            def prep(b):
                for c in range(TJ):
                    if c < 2:
                        if c == 0:
                            wait_apart(sp, pv_done, b * QT * STEPS + PR)
                            sp.wait_ge(den_done, b * QT * PAIRS + 1)
                        load_x(b, c)
                    load_adj(b, 0, c, Use(b, "prep", c - 1, "M") if c else None)
                    sp.wait_ge(hres_made, b * TJ + c + 1)
                    sp.dma_start(h_dram[b, c * T:(c + 1) * T, :].rearrange("(j p) d -> p j d", p=P), h_buf[c % 2]) \
                        .then_inc(h_stored[c % 2], 16)
                    if c + 2 < TJ:
                        sp.wait_ge(h_stored[c % 2], 16 * (b * 2 + c // 2 + 1))
                        load_x(b, c + 2)
                    for o in range(2):
                        sp.wait_ge(low_ready, b * 2 * TJ + 2 * c + o + 1 + 1)
                        for part, src in enumerate((high[o], low[o])):
                            sp.dma_start(qk_dram[b, part, o, :, c * T:(c + 1) * T]
                                         .rearrange("(g p) t -> p g t", p=P), src).then_inc(qk_stored[o], 16)
                        sp.dma_start(qk32_dram[b, o, :, c * T:(c + 1) * T].rearrange("(g p) t -> p g t", p=P),
                                     qk32[o]).then_inc(qk_stored[o], 16)
                    sp.wait_ge(qk_stored[1], 48 * (b * TJ + c + 1) + 1)
                    for r in range(4):
                        sp.dma_start(k_stack[DH * r:DH * (r + 1), :, c * T:(c + 1) * T],
                                     qk_dram[b, r % 2, 1, :, c * T:(c + 1) * T]
                                     .rearrange("(h d) t -> d h t", d=DH)).then_inc(k_loaded, 16)

            def load_q(b, q, g):
                for r in range(4):
                    sp.dma_start(q_stack[DH * r:DH * (r + 1), HG * g:HG * (g + 1), :],
                                 qk_dram[b, r // 2, 0, P * g:P * (g + 1), bass.ds(q * T, T)]
                                 .rearrange("(h d) t -> d h t", d=DH)).then_inc(q_loaded[g], 16)

            def load_residuals(b, q, n):
                sp.wait_ge(out_made, n + 1)
                sp.dma_start(y[:], h_dram[b, bass.ds(q * T, T), :].rearrange("(j p) d -> p j d", p=P)) \
                    .then_inc(y_loaded, 16)

            def load_x_again(b, q, last_use):
                last_use.wait_filled(sp)
                sp.dma_start(x_res, x[b, bass.ds(q * T, T), :].rearrange("(j p) d -> p j d", p=P)) \
                    .then_inc(xres_loaded, 16)

            def store_out(b, q, n):
                sp.wait_ge(out_made, n + 1 + 1)
                sp.dma_start(out[b, bass.ds(q * T, T), :].rearrange("(j p) d -> p j d", p=P), z[:]) \
                    .then_inc(out_stored, 16)

            def unit(b, q, kind, m):
                n = b * QT + q
                sp.wait_ge(pv_done, n * STEPS + PR)
                load_q(b, q, 1)
                if kind != "first":
                    load_residuals(b, q - 1, n - 1)
                if kind != "last":
                    load_adj(b, q + 1, 0, None)
                    load_adj(b, q + 1, 1, Use(b, kind, "M0", m=m))
                    load_adj(b, q + 1, 2, Use(b, kind, "M1", m=m))
                    Use(b, kind, KT - 1, 1, m=m).wait_filled(sp)
                    load_q(b, q + 1, 0)
                    load_adj(b, q + 1, 3, Use(b, kind, "M2", m=m))
                if kind != "first":
                    load_x_again(b, q - 1, Use(b, kind, "C3", m=m))
                    store_out(b, q - 1, n - 1)

            with sp.Fori(0, B) as b:
                prep(b)
                Use(b, "prep", TJ - 1, "V").wait_drained(sp)
                sp.dma_start(v_dram[b, :, :].rearrange("(k p) d -> p k d", p=P), v_sb[:]).then_inc(v_stored, 16)
                sp.wait_ge(qk_stored[0], 48 * (b * TJ + TJ) + 1)
                load_q(b, 0, 0)
                places(sp, b, unit)
                load_residuals(b, QT - 1, b * QT + QT - 1)
                load_x_again(b, QT - 1, Use(b, "post", "C3"))
                store_out(b, QT - 1, b * QT + QT - 1)
            def general_unit(b, q, u, n):
                t = u * GENERAL
                wait_apart(sp, out_stored, 16 * n + 1)
                for piece in range(TJ):
                    sp.wait_ge(turn, t + piece * PIECE + 1)
                    sp.dma_start(adj_rows[:], adj[b, piece * T:(piece + 1) * T, bass.ds(q * T, T)]
                                 .rearrange("(j p) t -> p j t", p=P)).then_inc(turn, 16)
                    sp.wait_ge(turn, t + piece * PIECE + 16 + 1)
                    sp.dma_start(adj_cols[:], adj[b, bass.ds(q * T, T), piece * T:(piece + 1) * T]
                                 .rearrange("(j p) t -> p j t", p=P)).then_inc(turn, 16)
                with sp.Fori(0, H) as h:
                    th = t + MASKED + h * HEAD
                    sp.wait_ge(turn, th + 1)
                    sp.dma_start(gen_q, qk32_dram[b, 0, bass.ds(h * DH, DH), bass.ds(q * T, T)]).then_inc(turn, 16)
                    sp.wait_ge(turn, th + 16 + 1)
                    sp.dma_start(gen_k, qk32_dram[b, 1, bass.ds(h * DH, DH), :]).then_inc(turn, 16)
                    sp.wait_ge(turn, th + 32 + 1)
                    with nc.allow_non_contiguous_dma(reason="one head of V"):
                        sp.dma_start(gen_v, v_dram[b, :, bass.ds(h * DH, DH)].rearrange("(k p) d -> p k d", p=P)) \
                            .then_inc(turn, 16)
                    sp.wait_ge(turn, th + HEAD - 16 + 1)
                    sp.dma_start(ctx_dram[bass.ds(h * DH, DH), :], gen_out[0:DH, :]).then_inc(turn, 16)
                sp.wait_ge(turn, t + GENERAL - 16 + 1)
                sp.dma_start(gen_ctxT, ctx_dram.rearrange("(g p) t -> p g t", p=P)).then_inc(turn, 16)
                load_residuals(b, q, n)
                load_x_again(b, q, GeneralUse(u, "C3"))
                store_out(b, q, n)
                wait_apart(sp, out_stored, 16 * (n + 1) + 1)

            sp.wait_ge(out_stored, 16 * B * QT + 1)
            sp.wait_ge(v_stored, 16 * B + 1)
            general(sp, general_unit)
            for i in range(2):
                sp.wait_ge(h_stored[i], 16 * 2 * B)
                sp.wait_ge(qk_stored[i], 48 * TJ * B + 1)

        @block.tensor
        def _(pe):
            pe.wait_ge(consts_made, 8)
            pe.wait_ge(weights_loaded, 16 * N_WEIGHTS)
            pe.wait_ge(bv_spread, 2)
            for k in range(KD):
                mm = pe.matmul(ctx_ps[:, 0:D], yT[:, k, 0:P], wo_sb[:, k, :], start=(k == 0), stop=(k == KD - 1))
            mm.then_inc(setup_full, 1)
            pe.wait_ge(bo_made, 1)

            def take(use):
                pe.wait_ge(drained[use.slot], use.before + 1)

            def mask_transposes(use, n, piece):
                take(use)
                pe.wait_ge(cols_signed, n * TJ + piece + 1 + 1)
                tile = use.tile[:].rearrange("p a t -> p (a t)").bitcast(BF16).rearrange("p (k t) -> p k t", t=T)
                for k in range(TJ):
                    for j in range(TJ):
                        mm = pe.transpose(tile[:, k, j * P:(j + 1) * P], cols_sign[:, j, k * P:(k + 1) * P],
                                          ident16[:])
                mm.then_inc(filled, 1)

            def prep(b):
                for c in range(TJ):
                    use = Use(b, "prep", c, "T")
                    take(use)
                    pe.wait_ge(h_ready, b * TJ + c + 1)
                    for k in range(KD):
                        for j in range(TJ):
                            mm = pe.transpose(use.tile[:, k, j * P:(j + 1) * P],
                                              h_buf[c % 2][:, j, k * P:(k + 1) * P], ident[:])
                    mm.then_inc(filled, 1)
                    for o, tag in enumerate("QK"):
                        use = Use(b, "prep", c, tag)
                        take(use)
                        Use(b, "prep", c, "T").wait_drained(pe)
                        for g in range(G):
                            for k in range(KD):
                                mm = pe.matmul(use.tile[:, g, :], wqkv_sb[:, k, o * D + g * P:o * D + (g + 1) * P],
                                               hT[:, k, :], start=(k == 0), stop=(k == KD - 1))
                        mm.then_inc(filled, 1)
                    use = Use(b, "prep", c, "V")
                    take(use)
                    for j in range(TJ):
                        for k in range(KD):
                            mm = pe.matmul(bank2(use.slot, D)[:, j, :], hT[:, k, j * P:(j + 1) * P],
                                           wqkv_sb[:, k, 2 * D:3 * D], start=(k == 0), stop=(k == KD - 1))
                    mm.then_inc(filled, 1)
                    for o, tag in enumerate(("NQ", "NK")):
                        use = Use(b, "prep", c, tag)
                        take(use)
                        pe.wait_ge(square_ready, b * 2 * TJ + 2 * c + o + 1 + 1)
                        for g in range(G):
                            mm = pe.matmul(use.tile[:, g, :], head_ones[:], square[o][:, g, :], start=True, stop=True)
                        mm.then_inc(filled, 1)
                    mask_transposes(Use(b, "prep", c, "M"), b * QT, c)

            def scores(b, q, kind, m, i):
                g, kt = divmod(i, KT)
                n = b * QT + q
                if kt == 0:
                    pe.wait_ge(q_loaded[g], 64 * (n + 1))
                if i == 0 and kind == "first":
                    pe.wait_ge(k_loaded, 64 * TJ * (b + 1))
                    Use(b, "prep", TJ - 1, "V").wait_drained(pe)
                for half in range(2):
                    use = Use(b, kind, i, half, m=m)
                    take(use)
                    for e in range(2):
                        h = HG * g + 2 * half + e
                        mm = pe.matmul(use.tile[:, e, :], k_stack[:, h, kt * P:(kt + 1) * P], q_stack[:, h, :],
                                       start=True, stop=True)
                    mm.then_inc(filled, 1)

            def denominators(n, m):
                pe.wait_ge(pairs_ready, n * PAIRS + m + 1 + 2)
                k = m % (KT // 2)
                for j in range(HG):
                    mm = pe.matmul(den_ps[DH * j:DH * (j + 1), :], ones[:, 0:DH], pairs[:, m % 2, j, :],
                                   start=(k == 0), stop=(k == KT // 2 - 1))
                mm.then_inc(den_done, 1)

            def weighted_values(n, i, probs_made):
                g, kt = divmod(i, KT)
                probs_made.wait_drained(pe)
                if kt == 0:
                    pe.wait_ge(ctx_ready, n * G + g + 1)
                for j in range(HG):
                    h = HG * g + j
                    mm = pe.matmul(ctx_ps[DH * j:DH * (j + 1), :], v_sb[:, kt, DH * h:DH * (h + 1)],
                                   probs[:, i % PR, j, :], start=(kt == 0), stop=(kt == KT - 1))
                mm.then_inc(pv_done, 1)

            def post(tag, n, where):
                use = where(tag)
                take(use)
                if tag == "A":
                    pe.wait_ge(ctx_ready, G * (n + 1) + 1)
                    for j in range(TJ):
                        for g in range(G):
                            mm = pe.matmul(bank2(use.slot, D)[:, j, :], ctxT[:, g, j * P:(j + 1) * P],
                                           wo_sb[:, g, :], start=(g == 0), stop=(g == G - 1))
                    mm.then_inc(filled, 1)
                elif tag == "B":
                    pe.wait_ge(y_ready, n + 1)
                    for k in range(KD):
                        for j in range(TJ):
                            mm = pe.transpose(use.tile[:, k, j * P:(j + 1) * P], y[:, j, k * P:(k + 1) * P], ident[:])
                    mm.then_inc(filled, 1)
                elif tag[0] == "C":
                    where("B").wait_drained(pe)
                    for e in range(2):
                        c = 2 * int(tag[1]) + e
                        for k in range(KD):
                            mm = pe.matmul(use.tile[:, e, :], w1_sb[:, k, c * P:(c + 1) * P], yT[:, k, :],
                                           start=(k == 0), stop=(k == KD - 1))
                    mm.then_inc(filled, 1)
                else:
                    j = int(tag[1])
                    where("C3").wait_drained(pe)
                    for c in range(FC):
                        mm = pe.matmul(use.tile[:, 0, 0:D], mlp[:, c, j * P:(j + 1) * P], w2_sb[:, c, :],
                                       start=(c == 0), stop=(c == FC - 1))
                    mm.then_inc(filled, 1)

            def unit(b, q, kind, m):
                n = b * QT + q
                for i in range(STEPS + LAG):
                    if i < STEPS:
                        scores(b, q, kind, m, i)
                        for tag in at(i, *([POST_PE] if kind != "first" else []), *([MASK_PE] if kind != "last" else [])):
                            use = Use(b, kind, tag, m=m)
                            if tag[0] == "M":
                                mask_transposes(use, n + 1, int(tag[1]))
                            else:
                                post(tag, n - 1, lambda t: Use(b, kind, t, m=m))
                    if i >= 4 and i % 2 == 0:
                        denominators(n, (i - 4) // 2)
                    if i >= LAG:
                        weighted_values(n, i - LAG, Use(b, kind, i - LAG, 1, m=m))
                denominators(n, PAIRS - 1)

            with pe.Fori(0, B) as b:
                prep(b)
                places(pe, b, unit)
                for tag in POST_TAGS:
                    post(tag, b * QT + QT - 1, lambda t: Use(b, "post", t))

            def general_unit(b, q, u, n):
                t = u * GENERAL
                turned = ring[0][:].rearrange("p a t -> p (a t)").bitcast(BF16).rearrange("p (k t) -> p k t", t=T)
                for piece in range(TJ):
                    pe.wait_ge(turn, t + piece * PIECE + 33 + 1)
                    for k in range(TJ):
                        for j in range(TJ):
                            mm = pe.transpose(turned[:, k, j * P:(j + 1) * P], cols_sign[:, j, k * P:(k + 1) * P],
                                              ident16[:])
                    mm.then_inc(turn, 1)
                with pe.Fori(0, H) as h:
                    th = t + MASKED + h * HEAD
                    with pe.Fori(0, KT) as k:
                        pe.wait_ge(turn, th + 51 + k * PASS1 + 1 + 1)
                        pe.matmul(ctx_ps[:], gen_k_tile, gen_q, start=True, stop=True).then_inc(turn, 1)
                    with pe.Fori(0, KT) as k:
                        tk = th + SUMS + k * PASS2
                        pe.wait_ge(turn, tk + 2 + 1)
                        pe.matmul(ctx_ps[:], gen_k_tile, gen_q, start=True, stop=True).then_inc(turn, 1)
                        pe.wait_ge(turn, tk + 7 + 1)
                        pe.matmul(den_ps[0:DH, :], gen_v_tile, gen_s, start=True, stop=True)
                        pe.matmul(ring[0][0:DH, 0, :], ones[:, 0:DH], gen_s, start=True, stop=True).then_inc(turn, 1)
                for tag in POST_TAGS:
                    post(tag, n, lambda t: GeneralUse(u, t))

            general(pe, general_unit)

        @block.scalar
        def _(act):
            act.wait_ge(weights_loaded, 16 * N_WEIGHTS)
            act.mul(qk_bias[:], qk_bias[:], QK_SCALE).then_inc(bias_scaled, 1)
            act.wait_ge(bias_scaled, 1)

            def sign(n, piece, before):
                act.wait_ge(cols_loaded, 16 * (n * TJ + piece + 1))
                if piece:
                    before.wait_filled(act)
                else:
                    act.wait_ge(mask_ready, n + 1)
                act.activation(cols_sign[:], adj_cols[:], ACT.Sign).then_inc(cols_signed, 1)

            def prep(b):
                sign(b * QT, 0, None)
                for c in range(TJ):
                    use = Use(b, "prep", c, "T")
                    use.wait_filled(act)
                    if c:
                        act.wait_ge(filled, Use(b, "prep", c - 1, "V").count)
                    act.activation(hT, use.tile[:], ACT.Copy).then_inc(drained[use.slot], 1)
                    for o, tag in enumerate("QK"):
                        use = Use(b, "prep", c, tag)
                        use.wait_filled(act)
                        act.wait_ge(low_ready, (b * 2 * TJ + 2 * c + o - 1 if c else b * 2 * TJ) + 1)
                        act.wait_ge(qk_stored[o], 48 * (b * TJ + c) + 1)
                        act.wait_ge(square_ready, (b * 2 * TJ + 2 * c + o - 1 if c else b * 2 * TJ) + 1)
                        for g in range(G):
                            a = act.activation(qk32[o][:, g, :], use.tile[:, g, :], ACT.Identity,
                                               bias=qk_bias[:, o * G + g:o * G + g + 1], scale=QK_SCALE)
                        a \
                        .then_inc(drained[use.slot], 1)
                    use = Use(b, "prep", c, "V")
                    use.wait_filled(act)
                    if c == 0:
                        act.wait_ge(v_stored, 16 * b + 1)
                    act.activation(v_sb[:, c * TJ:(c + 1) * TJ, :], bank2(use.slot, D), ACT.Copy) \
                        .then_inc(drained[use.slot], 1)
                    if c + 1 < TJ:
                        sign(b * QT, c + 1, Use(b, "prep", c, "M"))

            def post(tag, use, n):
                use.wait_filled(act)
                if tag == "B":
                    act.wait_ge(out_made, n + 1)
                    act.activation(yT[:], use.tile[:], ACT.Copy) \
                        .then_inc(drained[use.slot], 1)
                else:
                    for e in range(2):
                        c = 2 * int(tag[1]) + e
                        a = act.activation(mlp[:, c, :], use.tile[:, e, :], ACT.Relu, bias=mlp_bias[:, c:c + 1])
                    a \
                        .then_inc(drained[use.slot], 1)

            def unit(b, q, kind, m):
                n = b * QT + q
                for i in range(STEPS):
                    for half in range(2):
                        use = Use(b, kind, i, half, m=m)
                        use.wait_filled(act)
                        act.activation(use.tile[:], use.tile[:], ACT.Exp, scale=EXP_SCALE).then_inc(exp_done, 1)
                    for tag in at(i, *([POST_ACT] if kind != "first" else []), *([MASK_ACT] if kind != "last" else [])):
                        if tag[0] == "S":
                            piece = int(tag[1])
                            sign(n + 1, piece, Use(b, kind, f"M{piece - 1}", m=m) if piece else None)
                        else:
                            post(tag, Use(b, kind, tag, m=m), n - 1)

            with act.Fori(0, B) as b:
                prep(b)
                places(act, b, unit)
                for tag in POST_ACT:
                    post(tag, Use(b, "post", tag), b * QT + QT - 1)

            def general_unit(b, q, u, n):
                t = u * GENERAL
                for piece in range(TJ):
                    act.wait_ge(turn, t + piece * PIECE + 32 + 1)
                    act.activation(cols_sign[:], adj_cols[:], ACT.Sign).then_inc(turn, 1)
                with act.Fori(0, H) as h:
                    with act.Fori(0, KT) as k:
                        act.wait_ge(turn, t + MASKED + h * HEAD + SUMS + k * PASS2 + 5 + 1)
                        act.activation(gen_s, gen_s, ACT.Exp, scale=EXP_SCALE).then_inc(turn, 1)
                for tag in POST_ACT:
                    post(tag, GeneralUse(u, tag), n)

            general(act, general_unit)

        @block.vector
        def _(dve):
            dve.memset(ones[:], 1.0).then_inc(consts_made, 1)
            dve.memset(minus_half[:], -0.5).then_inc(half_made, 1)
            dve.memset(head_ones[:], 0.0).then_inc(consts_made, 1)
            dve.wait_ge(consts_made, 3)
            for j in range(HG):
                dve.memset(head_ones[DH * j:DH * (j + 1), DH * j:DH * (j + 1)], 1.0).then_inc(consts_made, 1)
            dve.wait_ge(weights_loaded, 16 * N_WEIGHTS)
            for k in range(KD):
                dve.tensor_scalar(yT[:, k, 0:P], ones[:], v_bias[:, k:k + 1], None, ALU.mult).then_inc(bv_spread, 1)
            dve.wait_ge(setup_full, 1)
            dve.tensor_tensor(rows[:, 5, :], rows[:, 5, :], ctx_ps[:, 0:D], ALU.add).then_inc(bo_made, 1)

            def mean_and_variance(stats_made, count, aggregated, veps_made, before):
                wait_apart(dve, stats_made, count)
                for j in range(TJ):
                    a = dve.bn_aggr(mean_var[:, j, :], stats[:, j, :])
                a.then_inc(aggregated, 1)
                dve.wait_ge(aggregated, before + 1)
                dve.tensor_scalar(var_eps[:], mean_var[:, :, 1], EPS, None, ALU.add).then_inc(veps_made, 1)

            def normalise(t, made):
                for j in range(TJ):
                    a = dve.tensor_scalar(t[:, j, :], t[:, j, :], mean_var[:, j, 0:1], rstd[:, j:j + 1],
                                          ALU.subtract, ALU.mult)
                a.then_inc(made, 1)

            def mask_from(use, n, buf, piece):
                k = n * TJ + piece
                use.wait_filled(dve)
                dve.wait_ge(rows_loaded, 16 * (k + 1))
                turned = use.tile[:].rearrange("p a t -> p (a t)").bitcast(BF16)
                rows_flat = adj_rows[:].rearrange("p j t -> p (j t)")
                dst = mask[:, bass.ds(buf * KT + piece * TJ, TJ), :].rearrange("p k t -> p (k t)")
                dve.scalar_tensor_tensor(out=dst, in0=rows_flat, scalar=0.0, in1=turned, op0=ALU.is_gt, op1=ALU.max) \
                        .then_inc(drained[use.slot], 1)

            def mask_diagonal(q, buf, last_piece):
                last_piece.wait_drained(dve)
                for j in range(TJ):
                    tile = mask[:, bass.ds(buf * KT + q * TJ + j, 1), j * P:(j + 1) * P].rearrange("p a t -> p (a t)")
                    a = dve.tensor_tensor(tile, tile, ident16[:], ALU.max)
                a.then_inc(mask_ready, 1)

            def prep_norm(b, c):
                n = b * TJ + c
                t = h_buf[c % 2]
                dve.wait_ge(x_loaded[c % 2], 16 * (b * 2 + c // 2 + 1))
                for j in range(TJ):
                    a = dve.bn_stats(stats[:, j, :], t[:, j, :])
                a.then_inc(prep_stats, 1)
                mean_and_variance(prep_stats, n + 1, prep_meanvar, prep_veps, n)
                dve.wait_ge(prep_rstd, n + 1)
                normalise(t, prep_normed)
                dve.wait_ge(prep_normed, n + 1)
                dve.tensor_scalar(t, t, 0.0, None, ALU.max).then_inc(h_ready, 1)

            def prep(b):
                prep_norm(b, 0)
                for c in range(TJ):
                    for o in range(2):
                        n = b * 2 * TJ + 2 * c + o
                        Use(b, "prep", c, "QK"[o]).wait_drained(dve)
                        dve.wait_ge(qk_stored[o], 48 * (b * TJ + c) + 1)
                        dve.tensor_copy(high[o], qk32[o]).then_inc(high_ready, 1)
                        dve.wait_ge(high_ready, n + 1)
                        dve.tensor_tensor(low[o], qk32[o], high[o], ALU.subtract).then_inc(low_ready, 1)
                    if c + 1 < TJ:
                        prep_norm(b, c + 1)
                    for o, tag in enumerate(("NQ", "NK")):
                        use = Use(b, "prep", c, tag)
                        use.wait_filled(dve)
                        dve.tensor_reduce((norms_q, norms_k)[o][:, bass.ds(b, 1), c * G:(c + 1) * G]
                                          .rearrange("p a g -> p (a g)"), use.tile[:], AX.X, ALU.max) \
                        .then_inc(drained[use.slot], 1)
                    mask_from(Use(b, "prep", c, "M"), b * QT, 0, c)
                mask_diagonal(0, 0, Use(b, "prep", TJ - 1, "M"))

            def masked(b, q, kind, m, i):
                kt = i % KT
                n = b * QT + q
                if i == 0:
                    dve.wait_ge(mask_ready, n + 1 + 1)
                dve.wait_ge(pv_done, n * STEPS + i + 1)
                dve.wait_ge(pairs_ready, n * PAIRS + i // 2 + 1)
                buf = {"first": 0, "middle": 1 - m, "last": (QT - 1) % 2}[kind]
                for half in range(2):
                    use = Use(b, kind, i, half, m=m)
                    if i + half:
                        dve.wait_ge(exp_done, n * 2 * STEPS + 2 * i + half + 1)
                    else:
                        wait_apart(dve, exp_done, n * 2 * STEPS + 1)
                    keep = mask[:, bass.ds(buf * KT + kt, 1), :]
                    dve.tensor_tensor(probs[:, i % PR, 2 * half:2 * half + 2, :], use.tile[:],
                                      keep.to_broadcast([P, 2, T]), ALU.mult) \
                        .then_inc(drained[use.slot], 1)

            def context(n, g):
                dve.wait_ge(den_done, n * PAIRS + (g + 1) * (KT // 2) + 1)
                dve.wait_ge(pv_done, n * STEPS + (g + 1) * KT + PR)
                dve.reciprocal(rden[:], den_ps[:]).then_inc(rden_ready, 1)
                dve.wait_ge(rden_ready, n * G + g + 1)
                dve.wait_ge(y_stats, n + 1)
                dve.tensor_tensor(ctxT[:, g, :], ctx_ps[:], rden[:], ALU.mult).then_inc(ctx_ready, 1)

            def post(tag, use, n):
                if tag == "A":
                    use.wait_filled(dve)
                    dve.wait_ge(y_loaded, 16 * (n + 1))
                    dve.tensor_tensor(y[:], bank2(use.slot, D), y[:], ALU.add) \
                        .then_inc(drained[use.slot], 1)
                    use.wait_drained(dve)
                    for j in range(TJ):
                        a = dve.bn_stats(stats[:, j, :], y[:, j, :])
                    a.then_inc(y_stats, 1)
                    mean_and_variance(y_stats, n + 2, y_meanvar, y_veps, n)
                elif tag == "N1":
                    dve.wait_ge(y_rstd, n + 1)
                    normalise(y, y_normed)
                elif tag[0] == "D":
                    j = int(tag[1])
                    use.wait_filled(dve)
                    dve.wait_ge(z_ready, n + 1)
                    dve.tensor_tensor(z[:, j, :], use.tile[:, 0, 0:D], z[:, j, :], ALU.add) \
                        .then_inc(drained[use.slot], 1)
                    use.wait_drained(dve)
                    dve.bn_stats(stats[:, j, :], z[:, j, :]).then_inc(z_stats, 1)
                    if tag == "D3":
                        mean_and_variance(z_stats, (n + 1) * TJ, z_meanvar, z_veps, n)
                elif tag == "N2":
                    dve.wait_ge(z_rstd, n + 1)
                    normalise(z, z_normed)
                elif tag == "OUT":
                    dve.wait_ge(z_shifted, n + 1)
                    dve.wait_ge(xres_loaded, 16 * (n + 1))
                    dve.tensor_tensor(z[:], z[:], x_res, ALU.add).then_inc(out_made, 1)

            def unit(b, q, kind, m):
                n = b * QT + q
                for i in range(STEPS):
                    masked(b, q, kind, m, i)
                    if i == KT + 1:
                        context(n, 0)
                    for tag in at(i, *([POST_DVE] if kind != "first" else []), *([MASK_DVE] if kind != "last" else [])):
                        use = Use(b, kind, tag, m=m) if tag in RING_TAGS else None
                        nxt = {"first": 1, "middle": m}.get(kind)
                        if tag[0] == "M":
                            mask_from(use, n + 1, nxt, int(tag[1]))
                        elif tag == "EYE":
                            mask_diagonal(q + 1, nxt, Use(b, kind, "M3", m=m))
                        else:
                            post(tag, use, n - 1)
                context(n, 1)

            with dve.Fori(0, B) as b:
                prep(b)
                places(dve, b, unit)
                for tag in POST_DVE:
                    post(tag, Use(b, "post", tag) if tag in RING_TAGS else None, b * QT + QT - 1)

            Use(B - 1, "prep", TJ - 1, "NK").wait_drained(dve)
            dve.tensor_tensor(products[:], norms_q[:], norms_k[:], ALU.mult).then_inc(products_made, 1)
            dve.wait_ge(products_made, 1)
            dve.tensor_scalar(products[:], products[:], SAFE_PRODUCT, None, ALU.is_le).then_inc(products_made, 1)
            dve.tensor_scalar(norms_q[:], norms_q[:], SAFE_NORM, None, ALU.is_le).then_inc(products_made, 1)
            dve.tensor_scalar(norms_k[:], norms_k[:], SAFE_NORM, None, ALU.is_le).then_inc(products_made, 1)
            dve.wait_ge(products_made, 4)
            for i, t in enumerate((products, norms_q, norms_k)):
                dve.tensor_reduce(unsafe[:, i:i + 1], t[:].rearrange("p b n -> p (b n)"), AX.X, ALU.min) \
                    .then_inc(products_made, 1)
            dve.wait_ge(products_made, 7)
            dve.tensor_reduce(unsafe[:, 3:4], unsafe[:, 0:3], AX.X, ALU.min).then_inc(products_made, 1)
            dve.wait_ge(products_made, 8)
            dve.tensor_scalar(unsafe[:, 0:1], unsafe[:, 3:4], -1.0, 1.0, ALU.mult, ALU.add).then_inc(products_made, 1)
            dve.wait_ge(flag_spread, 1)
            dve.tensor_copy(unsafe_int[:], unsafe[:, 1:2]).then_inc(flag_made, 1)

            def general_unit(b, q, u, n):
                t = u * GENERAL
                turned = ring[0][:].rearrange("p a t -> p (a t)").bitcast(BF16)
                for piece in range(TJ):
                    dve.wait_ge(turn, t + piece * PIECE + 34 + 1)
                    dve.scalar_tensor_tensor(
                        out=mask[:, piece * TJ:(piece + 1) * TJ, :].rearrange("p k t -> p (k t)"),
                        in0=adj_rows[:].rearrange("p j t -> p (j t)"), scalar=0.0, in1=turned,
                        op0=ALU.is_gt, op1=ALU.max).then_inc(turn, 1)
                dve.wait_ge(turn, t + MASKED - 1 + 1)
                for j in range(TJ):
                    tile = mask[:, bass.ds(q * TJ + j, 1), j * P:(j + 1) * P].rearrange("p a t -> p (a t)")
                    a = dve.tensor_tensor(tile, tile, ident16[:], ALU.max)
                a.then_inc(turn, 1)
                with dve.Fori(0, H) as h:
                    th = t + MASKED + h * HEAD
                    dve.wait_ge(turn, th + 48 + 1)
                    dve.memset(gen_max, LOWEST).then_inc(turn, 1)
                    dve.memset(gen_ctx, 0.0).then_inc(turn, 1)
                    dve.memset(gen_den, 0.0).then_inc(turn, 1)
                    with dve.Fori(0, KT) as k:
                        tk = th + 51 + k * PASS1
                        keep = mask[:, bass.ds(k, 1), :].rearrange("p a t -> p (a t)")
                        dve.wait_ge(turn, tk + 1)
                        dve.tensor_copy(gen_k_tile, gen_k[:, bass.ds(k * P, P)]).then_inc(turn, 1)
                        dve.wait_ge(turn, tk + 2 + 1)
                        dve.tensor_scalar(gen_bias, keep, -1.0, -LOWEST, ALU.add, ALU.mult).then_inc(turn, 1)
                        dve.wait_ge(turn, tk + 3 + 1)
                        dve.tensor_tensor(gen_s, ctx_ps[:], gen_bias, ALU.add).then_inc(turn, 1)
                        dve.wait_ge(turn, tk + 4 + 1)
                        dve.tensor_tensor(gen_max, gen_max, gen_s, ALU.max).then_inc(turn, 1)
                    with dve.Fori(0, KT) as k:
                        tk = th + SUMS + k * PASS2
                        keep = mask[:, bass.ds(k, 1), :].rearrange("p a t -> p (a t)")
                        dve.wait_ge(turn, tk + 1)
                        dve.tensor_copy(gen_k_tile, gen_k[:, bass.ds(k * P, P)]).then_inc(turn, 1)
                        dve.tensor_copy(gen_v_tile, gen_v[:, bass.ds(k, 1), :].rearrange("p a d -> p (a d)")) \
                            .then_inc(turn, 1)
                        dve.wait_ge(turn, tk + 3 + 1)
                        dve.tensor_tensor(gen_s, ctx_ps[:], gen_bias, ALU.subtract).then_inc(turn, 1)
                        dve.wait_ge(turn, tk + 4 + 1)
                        dve.tensor_scalar(gen_s, gen_s, 0.0, None, ALU.min).then_inc(turn, 1)
                        dve.wait_ge(turn, tk + 6 + 1)
                        dve.tensor_tensor(gen_s, gen_s, keep, ALU.mult).then_inc(turn, 1)
                        dve.wait_ge(turn, tk + 8 + 1)
                        dve.tensor_tensor(gen_ctx[0:DH, :], den_ps[0:DH, :], gen_ctx[0:DH, :], ALU.add) \
                            .then_inc(turn, 1)
                        dve.tensor_tensor(gen_den[0:DH, :], ring[0][0:DH, 0, :], gen_den[0:DH, :], ALU.add) \
                            .then_inc(turn, 1)
                    dve.wait_ge(turn, th + HEAD - 18 + 1)
                    dve.reciprocal(gen_den[0:DH, :], gen_den[0:DH, :]).then_inc(turn, 1)
                    dve.wait_ge(turn, th + HEAD - 17 + 1)
                    dve.tensor_tensor(gen_out[0:DH, :], gen_ctx[0:DH, :], gen_den[0:DH, :], ALU.mult) \
                        .then_inc(turn, 1)
                dve.wait_ge(turn, t + GENERAL + 1)
                for g in range(G):
                    dve.tensor_copy(ctxT[:, g, :], gen_ctxT[:, g, :]).then_inc(ctx_ready, 1)
                for tag in POST_DVE:
                    post(tag, GeneralUse(u, tag) if tag in RING_TAGS else None, n)

            general(dve, general_unit)

        @block.gpsimd
        def _(gp):
            gp.memset(ident[:], 0.0).then_inc(consts_made, 1)
            gp.wait_ge(consts_made, 3)
            gp.affine_select(out=ident[:], in_=ident[:], compare_op=ALU.not_equal, fill=1.0, base=0,
                             pattern=[[-1, P]], channel_multiplier=1).then_inc(consts_made, 1)
            gp.wait_ge(consts_made, 8)
            gp.tensor_copy(ident16[:], ident[:]).then_inc(consts_made, 1)
            for semaphore in (*drained, *qk_stored, mask_ready, cols_signed, out_made, out_stored, v_stored,
                              ctx_ready, den_done, y_stats, low_ready, square_ready, turn):
                gp.sem_inc(semaphore, 1)
            gp.sem_inc(pv_done, PR)
            gp.sem_inc(pairs_ready, 2)
            gp.wait_ge(half_made, 1)

            def row(i):
                return rows[:, i:i + 1, :].to_broadcast([P, TJ, D])

            def inverse_deviation(veps_made, made, n):
                gp.wait_ge(veps_made, n + 1)
                gp.tensor_tensor(rstd[:], var_eps[:], minus_half[:], ALU.pow).then_inc(made, 1)

            def prep(b):
                def squares(c):
                    for o in range(2):
                        n = b * 2 * TJ + 2 * c + o
                        Use(b, "prep", c, "QK"[o]).wait_drained(gp)
                        if c:
                            gp.wait_ge(filled, Use(b, "prep", c - 1, ("NQ", "NK")[o]).count)
                        gp.tensor_tensor(square[o], qk32[o], qk32[o], ALU.mult).then_inc(square_ready, 1)

                for c in range(TJ):
                    n = b * TJ + c
                    inverse_deviation(prep_veps, prep_rstd, n)
                    gp.wait_ge(h_ready, n + 1)
                    gp.wait_ge(filled, Use(b, "prep", c, "T").count)
                    gp.wait_ge(bo_made, 1)
                    gp.tensor_tensor(h_buf[c % 2], h_buf[c % 2], row(5), ALU.add).then_inc(hres_made, 1)
                    squares(c)

            def pair(n, m, probs_made):
                probs_made.wait_drained(gp)
                gp.wait_ge(den_done, (n * PAIRS + m - 1 if m >= 2 else n * PAIRS) + 1)
                a = (2 * m) % PR
                gp.tensor_tensor(pairs[:, m % 2], probs[:, a], probs[:, a + 1], ALU.add).then_inc(pairs_ready, 1)

            def post(tag, n):
                if tag == "R1":
                    inverse_deviation(y_veps, y_rstd, n)
                elif tag == "G1":
                    gp.wait_ge(y_normed, n + 1)
                    gp.tensor_tensor(y[:], y[:], row(0), ALU.mult).then_inc(y_scaled, 1)
                elif tag == "B1":
                    gp.wait_ge(y_scaled, n + 1)
                    gp.tensor_tensor(y[:], y[:], row(1), ALU.add).then_inc(y_ready, 1)
                elif tag == "X1":
                    gp.wait_ge(y_ready, n + 1)
                    gp.wait_ge(out_stored, 16 * n + 1)
                    gp.tensor_tensor(z[:], y[:], row(4), ALU.add).then_inc(z_ready, 1)
                elif tag == "R2":
                    inverse_deviation(z_veps, z_rstd, n)
                elif tag == "G2":
                    gp.wait_ge(z_normed, n + 1)
                    gp.tensor_tensor(z[:], z[:], row(2), ALU.mult).then_inc(z_scaled, 1)
                else:
                    gp.wait_ge(z_scaled, n + 1)
                    gp.tensor_tensor(z[:], z[:], row(3), ALU.add).then_inc(z_shifted, 1)

            def unit(b, q, kind, m):
                n = b * QT + q
                for i in range(STEPS):
                    if i % 2:
                        pair(n, i // 2, Use(b, kind, i, 1, m=m))
                    for tag in at(i, *([POST_POOL] if kind != "first" else [])):
                        post(tag, n - 1)

            with gp.Fori(0, B) as b:
                prep(b)
                places(gp, b, unit)
                for tag in POST_POOL:
                    post(tag, b * QT + QT - 1)

            gp.wait_ge(products_made, 9)
            gp.partition_all_reduce(unsafe[:, 1:2], unsafe[:, 0:1], P, RMAX).then_inc(flag_spread, 1)

            def general_unit(b, q, u, n):
                with gp.Fori(0, H) as h:
                    wait_apart(gp, turn, u * GENERAL + MASKED + h * HEAD + MAXIMUM + 1)
                    gp.partition_all_reduce(gen_bias, gen_max, P, RMAX).then_inc(turn, 1)
                for tag in POST_POOL:
                    post(tag, n)

            general(gp, general_unit)


def kernel(x, adj, L0_gnn_Wqkv, L0_gnn_bqkv, L0_gnn_Wo, L0_gnn_bo, L0_gnn_ln1_g, L0_gnn_ln1_b,
           L0_gnn_W1, L0_gnn_b1, L0_gnn_W2, L0_gnn_b2, L0_gnn_ln2_g, L0_gnn_ln2_b):
    import concourse.bacc as bacc
    from concourse.bass_utils import run_bass_kernel_spmd

    def flat(a):
        return np.ascontiguousarray(a)

    arrays = {
        "x": flat(x), "adj": flat(adj),
        "wqkvT": flat(np.asarray(L0_gnn_Wqkv).T), "bqkv": flat(L0_gnn_bqkv),
        "woT": flat(np.asarray(L0_gnn_Wo).T), "bo": flat(L0_gnn_bo),
        "g1": flat(L0_gnn_ln1_g), "b1n": flat(L0_gnn_ln1_b),
        "w1T": flat(np.asarray(L0_gnn_W1).T), "b1": flat(L0_gnn_b1),
        "w2T": flat(np.asarray(L0_gnn_W2).T), "b2": flat(L0_gnn_b2),
        "g2": flat(L0_gnn_ln2_g), "b2n": flat(L0_gnn_ln2_b),
    }
    nc = bacc.Bacc("TRN2", target_bir_lowering=False, num_devices=1)
    args = [nc.dram_tensor(f"in_{k}", a.shape, mybir.dt.from_np(a.dtype), kind="ExternalInput").ap()
            for k, a in arrays.items()]
    out = nc.dram_tensor("out", x.shape, F32, kind="ExternalOutput").ap()
    gnn_layer(nc, *args, out)
    r = run_bass_kernel_spmd(nc, [{f"in_{k}": a for k, a in arrays.items()}], core_ids=[0])
    return r.results[0]["out"]
```

```python
from contextlib import ExitStack

import numpy as np

import concourse.bass as bass
from concourse import mybir

F32 = mybir.dt.float32
F16 = mybir.dt.float16
BF16 = mybir.dt.bfloat16
I32 = mybir.dt.int32
U8 = mybir.dt.uint8
ALU = mybir.AluOpType
ACT = mybir.ActivationFunctionType
AX = mybir.AxisListType
RMAX = bass.bass_isa.ReduceOp.max

P = 128
D = 256
H = 8
DH = D // H
HG = P // DH
G = H // HG
F = 4 * D
FC = F // P
KD = D // P
T = 512
TJ = T // P
EPS = 1e-5
QK_SCALE = 64.0
SAFE_SCORE = 58.0
EXP_SCALE = 1.0 / (QK_SCALE * QK_SCALE * float(np.sqrt(DH)))
SAFE_PRODUCT = (SAFE_SCORE / EXP_SCALE) ** 2
SAFE_NORM = 6e4 ** 2
RING = 3
PR = 4
LAG = 3
DEN_LAG = 4
TAIL = LAG

POST_PE = {"A0": 7, "A1": 8, "B": 13, **{f"C{c}": 14 + c for c in range(FC)},
           **{f"D{d}": 22 + d for d in range(2 * TJ)}}
MASK_PE = {"M0": 4, "M1": 9, "M2": 12, "M3": 30}
POST_ACT = {tag: step for tag, step in POST_PE.items() if tag[0] in "BC"}
MASK_ACT = {"S0": 3, "S1": 8, "S2": 11, "S3": 20}
POST_DVE = {"A0": 7, "A1": 8, "N1": 10, "B1": 12,
            **{tag: step for tag, step in POST_PE.items() if tag[0] == "D"}, "N2": 31, "OUT": 31}
MASK_DVE = {**MASK_PE, "EYE": 31}
POST_POOL = {"R1": 9, "G1": 10, "X1": 14, "R2": 30}
POST_TAGS = tuple(POST_PE)
RING_TAGS = POST_TAGS + tuple(MASK_PE)
C_END = f"C{FC - 1}"
NEXT_DVE = {"stat0": 30, "norm0": 31}
NEXT_POOL = {"pow0": 31}

TURN_PE = """T0 Q0 A0 K0 A1 V0 T1 NQ0 NK0 Q1 B C0 K1 C1 C2 V1 C3 C4 T2 NQ1 NK1 Q2 C5 C6 K2 C7 D0 V2 D1 D2
             T3 NQ2 NK2 Q3 D3 D4 K3 D5 D6 V3 D7 NQ3 NK3""".split()
TURN_DVE = """stat1 A0 HQ0 A1 norm1 N1 HK0 B1 NQ0 NK0 stat2 HQ1 norm2 HK1 NQ1 NK1 stat3 HQ2 norm3 HK2 D0 D1 D2
              NQ2 NK2 HQ3 D3 D4 HK3 D5 D6 D7 NQ3 NK3 N2 OUT""".split()
TURN_POOL = """pow1 res0 SQ0 R1 SK0 G1 res1 pow2 SQ1 X1 SK1 res2 pow3 SQ2 SK2 res3 SQ3 SK3 R2""".split()
TURN_ACT = [tag for tag in TURN_PE if tag[0] in "TQKVBC"]


def without_post(order):
    return [tag for tag in order if tag not in (*POST_DVE, *POST_POOL, *POST_TAGS)]


START_PE, START_DVE, START_ACT = [], ["stat0", "norm0"], ["S0"]
for tag in without_post(TURN_PE):
    START_PE += [tag, f"M{tag[2:]}"] if tag[:2] == "NK" else [tag]
for tag in without_post(TURN_DVE):
    START_DVE += [tag, f"M{tag[2:]}"] if tag[:2] == "NK" else [tag]
for tag in without_post(TURN_ACT):
    START_ACT += [tag, f"S{tag[1:]}"] if tag[0] == "Q" and tag != "Q0" else [tag]
START_POOL = ["pow0"] + without_post(TURN_POOL)


def at(step, *tables):
    return [tag for table in tables for tag, s in table.items() if s == step]


class Uses:

    def __init__(self, steps):
        self.steps = steps
        self.start, self.place, self.length = {"start": 0}, {}, {}
        for kind, order in (("start", START_PE), ("turn", TURN_PE), ("post", POST_TAGS)):
            for m, tag in enumerate(order):
                self.place[kind, tag] = m
            self.length[kind] = len(order)
        for kind, post, mask in (("first", 0, 1), ("middle", 1, 1), ("last", 1, 1), ("final", 1, 0)):
            m = 0
            for i in range(steps):
                tags = at(i, *([POST_PE] if post else []), *([MASK_PE] if mask else []))
                for key in ((i, 0), *((tag,) for tag in tags), (i, 1)):
                    self.place[(kind, *key)] = m
                    m += 1
            self.length[kind] = m
        self.middle = self.length["middle"]
        self.start["first"] = self.length["start"]
        self.start["middle"] = self.start["first"] + self.length["first"]
        self.start["last"] = self.start["final"] = self.start["middle"] + 2 * self.middle
        self.start["turn"] = self.start["last"] + self.length["last"]
        self.start["post"] = self.start["final"] + self.length["final"]
        self.total = self.start["turn"] + self.length["turn"] - self.start["first"]
        assert self.total == self.start["post"] + self.length["post"]
        assert self.total % RING == 0 and self.middle % RING == 0

    def of(self, kind, *key):
        return self.start[kind] + self.place[(kind, *key)]

    def of_unit_before(self, kind, *key):
        from_end = self.length["middle"] - self.place[("middle", *key)]
        assert from_end == self.length["first"] - self.place[("first", *key)]
        return self.start[kind] - from_end


def gnn_layer(nc, x, adj, wqkvT, bqkv, woT, bo, g1, b1n, w1T, b1, w2T, b2, g2, b2n, out):
    B, N, _ = x.shape
    KT = N // P
    QT = N // T
    STEPS = G * KT
    PAIRS = STEPS // 2
    assert QT == 4 and QT == TJ
    uses = Uses(STEPS)

    stack = ExitStack()
    with stack:
        def sb(name, shape, dt):
            return stack.enter_context(nc.sbuf_tensor(name, shape, dt))

        def sem(name):
            return stack.enter_context(nc.semaphore(name))

        def scratch(name, shape, dt):
            return nc.dram_tensor(name, shape, dt, kind="Internal").ap()

        h_dram = scratch("h_dram", (B, N, D), F32)
        qk_dram = scratch("qk_dram", (B, 2, 2, D, N), F16)
        qk32_dram = scratch("qk32_dram", (B, 2, D, N), F32)
        v_dram = scratch("v_dram", (B, N, D), F32)
        ctx_dram = scratch("ctx_dram", (D, T), F32)

        wqkv_sb = sb("wqkv_sb", [P, KD, 3 * D], F32)
        wo_sb = sb("wo_sb", [P, KD, D], F32)
        w1_sb = sb("w1_sb", [P, KD, F], F32)
        w2_sb = sb("w2_sb", [P, FC, D], F32)
        rows = sb("rows", [P, 6, D], F32)
        qk_bias = sb("qk_bias", [P, 2 * KD], F32)
        v_bias = sb("v_bias", [P, KD], F32)
        mlp_bias = sb("mlp_bias", [P, FC], F32)
        ones = sb("ones", [P, P], F32)
        ident = sb("ident", [P, P], F32)
        ident16 = sb("ident16", [P, P], BF16)
        head_ones = sb("head_ones", [P, P], BF16)
        minus_half = sb("minus_half", [P, TJ], F32)

        mask = sb("mask", [P, 2 * KT, T], U8)
        k_stack = sb("k_stack", [P, H, N], F16)
        q_stack = sb("q_stack", [P, H, T], F16)
        v_sb = sb("v_sb", [P, KT, D], F32)
        probs = sb("probs", [P, PR, HG, T], F32)
        pairs = sb("pairs", [P, 2, HG, T], F32)
        ctxT = sb("ctxT", [P, G, T], F32)
        rden = sb("rden", [P, T], F32)
        adj_rows = sb("adj_rows", [P, TJ, T], I32)
        adj_cols = sb("adj_cols", [P, TJ, T], I32)
        cols_sign = sb("cols_sign", [P, TJ, T], BF16)
        y = sb("y", [P, TJ, D], F32)
        z = sb("z", [P, TJ, D], F32)
        yT = sb("yT", [P, KD, T], F32)
        x_res = yT[:].rearrange("p k t -> p (k t)").rearrange("p (j d) -> p j d", d=D)
        mlp = sb("mlp", [P, FC, T], F32)
        stats, chunk_stats = (sb(name, [P, TJ, 6], F32) for name in ("stats", "chunk_stats"))
        mean_var, chunk_mean_var = (sb(name, [P, TJ, 2], F32) for name in ("mean_var", "chunk_mean_var"))
        var_eps, chunk_var_eps = (sb(name, [P, TJ], F32) for name in ("var_eps", "chunk_var_eps"))
        rstd, chunk_rstd = (sb(name, [P, TJ], F32) for name in ("rstd", "chunk_rstd"))

        pool = probs[:].rearrange("p a h t -> p (a h t)")

        def lent(offset, n, dt=F32):
            return pool[:, offset:offset + n].bitcast(dt) if dt != F32 else pool[:, offset:offset + n]

        W = TJ * D

        def h_buf(b, c):
            home = pool if isinstance(b, int) and b == 0 else adj_cols[:].rearrange("p j t -> p (j t)").bitcast(F32)
            return home[:, (c % 2) * W:(c % 2 + 1) * W].rearrange("p (j d) -> p j d", d=D)

        hT = lent(2 * W, W).rearrange("p (k t) -> p k t", t=T)
        qk32 = [lent((3 + i) * W, W).rearrange("p (g t) -> p g t", t=T) for i in range(2)]
        high = [lent(5 * W + i * W // 2, W // 2, F16).rearrange("p (g t) -> p g t", t=T) for i in range(2)]
        low = [lent(6 * W + i * W // 2, W // 2, F16).rearrange("p (g t) -> p g t", t=T) for i in range(2)]
        square = [lent(7 * W + i * W // 2, W // 2, BF16).rearrange("p (g t) -> p g t", t=T) for i in range(2)]
        norms_q = sb("norms_q", [P, B, G * TJ], F32)
        norms_k = sb("norms_k", [P, B, G * TJ], F32)
        products = sb("products", [P, B, G * TJ], F32)
        unsafe = sb("unsafe", [P, 4], F32)
        unsafe_int = sb("unsafe_int", [P, 1], I32)

        ring = [stack.enter_context(nc.psum_tensor(f"ring{i}", [P, 2, T], F32)) for i in range(RING)]
        ctx_ps = stack.enter_context(nc.psum_tensor("ctx_ps", [P, T], F32))
        den_ps = stack.enter_context(nc.psum_tensor("den_ps", [P, T], F32))

        filled = sem("filled")
        drained = [sem(f"drained{i}") for i in range(RING)]
        consts_made = sem("consts_made")
        half_made = sem("half_made")
        weights_loaded = sem("weights_loaded")
        bv_spread = sem("bv_spread")
        bo_made = sem("bo_made")
        bias_scaled = sem("bias_scaled")
        setup_full = sem("setup_full")
        x_loaded = [sem(f"x_loaded{i}") for i in range(2)]
        prep_stats = sem("prep_stats")
        prep_meanvar = sem("prep_meanvar")
        prep_veps = sem("prep_veps")
        prep_rstd = sem("prep_rstd")
        prep_normed = sem("prep_normed")
        h_ready = sem("h_ready")
        hres_made = sem("hres_made")
        h_stored = [sem(f"h_stored{i}") for i in range(2)]
        high_ready = sem("high_ready")
        low_ready = sem("low_ready")
        square_ready = sem("square_ready")
        qk_stored = [sem("q_stored"), sem("k_stored")]
        k_loaded = sem("k_loaded")
        v_stored = sem("v_stored")
        rows_loaded = sem("rows_loaded")
        cols_loaded = sem("cols_loaded")
        cols_signed = sem("cols_signed")
        mask_ready = sem("mask_ready")
        q_loaded = [sem(f"q_loaded{g}") for g in range(G)]
        exp_done = sem("exp_done")
        pairs_ready = sem("pairs_ready")
        pv_done = sem("pv_done")
        den_done = sem("den_done")
        ctx_copied = sem("ctx_copied")
        rden_ready = sem("rden_ready")
        ctx_ready = sem("ctx_ready")
        y_loaded = sem("y_loaded")
        xres_loaded = sem("xres_loaded")
        y_stats = sem("y_stats")
        y_meanvar = sem("y_meanvar")
        y_veps = sem("y_veps")
        y_rstd = sem("y_rstd")
        y_normed = sem("y_normed")
        y_scaled = sem("y_scaled")
        y_ready = sem("y_ready")
        z_ready = sem("z_ready")
        z_stats = sem("z_stats")
        z_meanvar = sem("z_meanvar")
        z_veps = sem("z_veps")
        z_rstd = sem("z_rstd")
        z_normed = sem("z_normed")
        z_scaled = sem("z_scaled")
        out_made = sem("out_made")
        out_stored = sem("out_stored")
        products_made = sem("products_made")
        flag_spread = sem("flag_spread")
        flag_made = sem("flag_made")
        turn = sem("turn")

        passed = sem("passed")

        def wait_apart(eng, semaphore, value):
            eng.wait_ge(semaphore, value)
            eng.sem_inc(passed, 1)

        N_WEIGHTS = 13

        def row(i):
            return rows[:, i:i + 1, :].to_broadcast([P, TJ, D])

        def bank2(slot, n):
            return ring[slot][:].rearrange("p a (c n) -> p (a c) n", n=n)

        class Use:

            def __init__(self, b, kind, *key, m=0, unit_before=False):
                u = uses.of_unit_before(kind, *key) if unit_before else uses.of(kind, *key)
                self.slot = u % RING
                per = uses.total // RING
                self.before = b * per + m * (uses.middle // RING) + u // RING
                self.count = b * uses.total + m * uses.middle + u + 1
                self.tile = ring[self.slot]

            def wait_filled(self, eng):
                eng.wait_ge(filled, self.count)

            def wait_drained(self, eng):
                eng.wait_ge(drained[self.slot], self.before + 1 + 1)

        PIECE = 35
        MASKED = TJ * PIECE + 1
        PASS1, PASS2 = 5, 10
        MAXIMUM = 51 + KT * PASS1
        SUMS = MAXIMUM + 1
        HEAD = SUMS + KT * PASS2 + 18
        GENERAL = MASKED + H * HEAD + 16
        LOWEST = -3e38
        flat = probs[:].rearrange("p a h t -> p (a h t)")
        gen_q = flat[0:DH, 0:T]
        gen_k = flat[0:DH, T:T + N]
        gen_v = flat[:, T + N:T + N + KT * DH].rearrange("p (k d) -> p k d", d=DH)
        o = T + N + KT * DH
        gen_k_tile, gen_v_tile = flat[0:DH, o:o + P], flat[:, o + P:o + P + DH]
        o += T
        gen_max, gen_s, gen_bias, gen_ctx, gen_den, gen_out = (
            flat[:, o + i * T:o + (i + 1) * T] for i in range(6))
        o += 6 * T
        gen_ctxT = flat[:, o:o + G * T].rearrange("p (g t) -> p g t", t=T)

        class GeneralUse:

            def __init__(self, u, tag):
                i = POST_TAGS.index(tag)
                self.slot = i % RING
                own = len(range(self.slot, len(POST_TAGS), RING))
                self.before = B * (uses.total // RING) + u * own + i // RING
                self.count = B * uses.total + u * len(POST_TAGS) + i + 1
                self.tile = ring[self.slot]

            wait_filled, wait_drained = Use.wait_filled, Use.wait_drained

        def general(eng, unit):
            eng.wait_ge(flag_made, 1)
            flag = eng.value_load(unsafe_int[0:1, 0:1])
            with eng.If(flag > 0):
                with eng.Fori(0, B) as b:
                    with eng.Fori(0, QT) as q:
                        u = b * QT + q
                        unit(b, q, u, u + B * QT)

        def program(eng, start, unit, between, post):
            start()
            if B > 1:
                with eng.Fori(0, B - 1) as b:
                    unit(b, 0, "first", 0)
                    with eng.Fori(0, QT - 2) as m:
                        unit(b, m + 1, "middle", m)
                    unit(b, QT - 1, "last", 0)
                    between(b)
            unit(B - 1, 0, "first", 0)
            with eng.Fori(0, QT - 2) as m:
                unit(B - 1, m + 1, "middle", m)
            unit(B - 1, QT - 1, "final", 0)
            post(B - 1)

        block = stack.enter_context(nc.Block())

        @block.sync
        def _(sp):
            for dst, src in (
                (wqkv_sb[:], wqkvT.rearrange("(k p) n -> p k n", p=P)),
                (wo_sb[:], woT.rearrange("(k p) n -> p k n", p=P)),
                (w1_sb[:], w1T.rearrange("(k p) n -> p k n", p=P)),
                (w2_sb[:], w2T.rearrange("(k p) n -> p k n", p=P)),
                (qk_bias[:], bqkv[0:2 * D].rearrange("(c p) -> p c", p=P)),
                (v_bias[:], bqkv[2 * D:3 * D].rearrange("(c p) -> p c", p=P)),
                (mlp_bias[:], b1.rearrange("(c p) -> p c", p=P)),
                *[(rows[:, i, :], v.partition_broadcast(P)) for i, v in enumerate((g1, b1n, g2, b2n, b2, bo))],
            ):
                with nc.allow_non_contiguous_dma(reason="small vectors, once"):
                    sp.dma_start(dst, src).then_inc(weights_loaded, 16)

            def load_x(b, c):
                sp.dma_start(h_buf(b, c), x[bass.ds(b, 1), c * T:(c + 1) * T, :]
                             .rearrange("a (j p) d -> p (a j) d", p=P)).then_inc(x_loaded[c % 2], 16)

            def load_adj(b, q, piece, before):
                n = b * QT + q
                if piece:
                    before.wait_drained(sp)
                else:
                    sp.wait_ge(mask_ready, n + 1)
                sp.dma_start(adj_rows[:], adj[b, piece * T:(piece + 1) * T, bass.ds(q * T, T)]
                             .rearrange("(j p) t -> p j t", p=P)).then_inc(rows_loaded, 16)
                sp.wait_ge(cols_signed, n * TJ + piece + 1)
                sp.dma_start(adj_cols[:], adj[b, bass.ds(q * T, T), piece * T:(piece + 1) * T]
                             .rearrange("(j p) t -> p j t", p=P)).then_inc(cols_loaded, 16)

            def store_residual(b, c):
                sp.wait_ge(hres_made, (b * TJ + c) + 1)
                sp.dma_start(h_dram[b, c * T:(c + 1) * T, :].rearrange("(j p) d -> p j d", p=P), h_buf(b, c)) \
                    .then_inc(h_stored[c % 2], 16)

            def store_parts(b, c, o):
                sp.wait_ge(low_ready, b * 2 * TJ + 2 * c + o + 1 + 1)
                for part, src in enumerate((high[o], low[o])):
                    sp.dma_start(qk_dram[b, part, o, :, c * T:(c + 1) * T]
                                 .rearrange("(g p) t -> p g t", p=P), src).then_inc(qk_stored[o], 16)
                sp.dma_start(qk32_dram[b, o, :, c * T:(c + 1) * T].rearrange("(g p) t -> p g t", p=P),
                             qk32[o]).then_inc(qk_stored[o], 16)

            def chunk(b, c):
                store_parts(b, c, 0)
                store_residual(b, c)
                store_parts(b, c, 1)
                if c + 2 < TJ:
                    sp.wait_ge(h_stored[c % 2], 16 * (b * 2 + c // 2 + 1))
                    load_x(b, c + 2)
                if c == 0:
                    sp.wait_ge(qk_stored[0], 48 * (b * TJ + 1) + 1)
                    for g in range(G):
                        load_q(b, 0, g)
                sp.wait_ge(qk_stored[1], 48 * (b * TJ + c + 1) + 1)
                for r in range(4):
                    sp.dma_start(k_stack[DH * r:DH * (r + 1), :, c * T:(c + 1) * T],
                                 qk_dram[b, r % 2, 1, :, c * T:(c + 1) * T]
                                 .rearrange("(h d) t -> d h t", d=DH)).then_inc(k_loaded, 16)

            def load_q(b, q, g):
                for r in range(4):
                    sp.dma_start(q_stack[DH * r:DH * (r + 1), HG * g:HG * (g + 1), :],
                                 qk_dram[b, r // 2, 0, P * g:P * (g + 1), bass.ds(q * T, T)]
                                 .rearrange("(h d) t -> d h t", d=DH)).then_inc(q_loaded[g], 16)

            def load_residuals(b, q, n):
                sp.wait_ge(out_made, n + 1)
                sp.dma_start(y[:], h_dram[b, bass.ds(q * T, T), :].rearrange("(j p) d -> p j d", p=P)) \
                    .then_inc(y_loaded, 16)

            def load_x_again(b, q, last_use):
                last_use.wait_filled(sp)
                sp.dma_start(x_res, x[b, bass.ds(q * T, T), :].rearrange("(j p) d -> p j d", p=P)) \
                    .then_inc(xres_loaded, 16)

            def store_out(b, q, n):
                sp.wait_ge(out_made, n + 1 + 1)
                sp.dma_start(out[b, bass.ds(q * T, T), :].rearrange("(j p) d -> p j d", p=P), z[:]) \
                    .then_inc(out_stored, 16)

            def unit(b, q, kind, m):
                n = b * QT + q
                bn, qn = (b + 1, 0) if kind == "last" else (b, q + 1)
                if kind != "final":
                    load_adj(bn, qn, 0, None)
                if kind == "first":
                    Use(b, kind, 0, 0).wait_filled(sp)
                    sp.dma_start(v_dram[b, :, :].rearrange("(k p) d -> p k d", p=P), v_sb[:]).then_inc(v_stored, 16)
                else:
                    sp.wait_ge(pv_done, n * STEPS + PR)
                    load_q(b, q, 1)
                    load_residuals(b, q - 1, n - 1)
                if kind != "final":
                    for piece in range(1, TJ):
                        load_adj(bn, qn, piece, Use(b, kind, f"M{piece - 1}", m=m))
                if kind == "last":
                    sp.wait_ge(cols_signed, (n + 2) * TJ + 1)
                    for c in range(2):
                        load_x(bn, c)
                elif kind != "final":
                    Use(b, kind, KT - 1, 1, m=m).wait_filled(sp)
                    load_q(b, q + 1, 0)
                if kind != "first":
                    load_x_again(b, q - 1, Use(b, kind, C_END, m=m))
                    store_out(b, q - 1, n - 1)

            def start():
                for c in range(2):
                    load_x(0, c)
                load_adj(0, 0, 0, None)
                for c in range(TJ):
                    chunk(0, c)
                    if c + 1 < TJ:
                        load_adj(0, 0, c + 1, Use(0, "start", f"M{c}"))

            def between(b):
                load_residuals(b, QT - 1, b * QT + QT - 1)
                for c in range(TJ):
                    if c == TJ - 1:
                        load_x_again(b, QT - 1, Use(b, "turn", C_END))
                    chunk(b + 1, c)
                for i in range(2):
                    sp.wait_ge(h_stored[i], 16 * 2 * (b + 2))
                store_out(b, QT - 1, b * QT + QT - 1)

            def post(b):
                load_residuals(b, QT - 1, b * QT + QT - 1)
                load_x_again(b, QT - 1, Use(b, "post", C_END))
                store_out(b, QT - 1, b * QT + QT - 1)

            program(sp, start, unit, between, post)

            def general_unit(b, q, u, n):
                t = u * GENERAL
                wait_apart(sp, out_stored, 16 * n + 1)
                for piece in range(TJ):
                    sp.wait_ge(turn, t + piece * PIECE + 1)
                    sp.dma_start(adj_rows[:], adj[b, piece * T:(piece + 1) * T, bass.ds(q * T, T)]
                                 .rearrange("(j p) t -> p j t", p=P)).then_inc(turn, 16)
                    sp.wait_ge(turn, t + piece * PIECE + 16 + 1)
                    sp.dma_start(adj_cols[:], adj[b, bass.ds(q * T, T), piece * T:(piece + 1) * T]
                                 .rearrange("(j p) t -> p j t", p=P)).then_inc(turn, 16)
                with sp.Fori(0, H) as h:
                    th = t + MASKED + h * HEAD
                    sp.wait_ge(turn, th + 1)
                    sp.dma_start(gen_q, qk32_dram[b, 0, bass.ds(h * DH, DH), bass.ds(q * T, T)]).then_inc(turn, 16)
                    sp.wait_ge(turn, th + 16 + 1)
                    sp.dma_start(gen_k, qk32_dram[b, 1, bass.ds(h * DH, DH), :]).then_inc(turn, 16)
                    sp.wait_ge(turn, th + 32 + 1)
                    with nc.allow_non_contiguous_dma(reason="one head of V"):
                        sp.dma_start(gen_v, v_dram[b, :, bass.ds(h * DH, DH)].rearrange("(k p) d -> p k d", p=P)) \
                            .then_inc(turn, 16)
                    sp.wait_ge(turn, th + HEAD - 16 + 1)
                    sp.dma_start(ctx_dram[bass.ds(h * DH, DH), :], gen_out[0:DH, :]).then_inc(turn, 16)
                sp.wait_ge(turn, t + GENERAL - 16 + 1)
                sp.dma_start(gen_ctxT, ctx_dram.rearrange("(g p) t -> p g t", p=P)).then_inc(turn, 16)
                load_residuals(b, q, n)
                load_x_again(b, q, GeneralUse(u, C_END))
                store_out(b, q, n)
                wait_apart(sp, out_stored, 16 * (n + 1) + 1)

            sp.wait_ge(out_stored, 16 * B * QT + 1)
            sp.wait_ge(v_stored, 16 * B + 1)
            general(sp, general_unit)
            for i in range(2):
                sp.wait_ge(h_stored[i], 16 * 2 * B)
                sp.wait_ge(qk_stored[i], 48 * TJ * B + 1)

        @block.tensor
        def _(pe):
            pe.wait_ge(consts_made, 8)
            pe.wait_ge(weights_loaded, 16 * N_WEIGHTS)
            pe.wait_ge(bv_spread, 2)
            for k in range(KD):
                mm = pe.matmul(ctx_ps[:, 0:D], yT[:, k, 0:P], wo_sb[:, k, :], start=(k == 0), stop=(k == KD - 1))
            mm.then_inc(setup_full, 1)
            pe.wait_ge(bo_made, 1)

            def take(use):
                pe.wait_ge(drained[use.slot], use.before + 1)

            def mask_transposes(use, n, piece):
                take(use)
                pe.wait_ge(cols_signed, n * TJ + piece + 1 + 1)
                tile = use.tile[:].rearrange("p a t -> p (a t)").bitcast(BF16).rearrange("p (k t) -> p k t", t=T)
                for k in range(TJ):
                    for j in range(TJ):
                        mm = pe.transpose(tile[:, k, j * P:(j + 1) * P], cols_sign[:, j, k * P:(k + 1) * P],
                                          ident16[:])
                mm.then_inc(filled, 1)

            def chunk(tag, b, where):
                use = where(tag)
                take(use)
                c = int(tag[-1])
                if tag[0] == "T":
                    pe.wait_ge(h_ready, b * TJ + c + 1)
                    for k in range(KD):
                        for j in range(TJ):
                            mm = pe.transpose(use.tile[:, k, j * P:(j + 1) * P],
                                              h_buf(b, c)[:, j, k * P:(k + 1) * P], ident[:])
                elif tag[0] in "QK":
                    where(f"T{c}").wait_drained(pe)
                    o = "QK".index(tag[0])
                    for g in range(G):
                        for k in range(KD):
                            mm = pe.matmul(use.tile[:, g, :], wqkv_sb[:, k, o * D + g * P:o * D + (g + 1) * P],
                                           hT[:, k, :], start=(k == 0), stop=(k == KD - 1))
                elif tag[0] == "V":
                    for j in range(TJ):
                        for k in range(KD):
                            mm = pe.matmul(bank2(use.slot, D)[:, j, :], hT[:, k, j * P:(j + 1) * P],
                                           wqkv_sb[:, k, 2 * D:3 * D], start=(k == 0), stop=(k == KD - 1))
                else:
                    o = "QK".index(tag[1])
                    pe.wait_ge(square_ready, b * 2 * TJ + 2 * c + o + 1 + 1)
                    for g in range(G):
                        mm = pe.matmul(use.tile[:, g, :], head_ones[:], square[o][:, g, :], start=True, stop=True)
                mm.then_inc(filled, 1)

            def scores(b, q, kind, m, i, half):
                g, kt = divmod(i, KT)
                if kt == 0 and half == 0:
                    pe.wait_ge(q_loaded[g], 64 * (b * QT + q + 1))
                if kind == "first" and g == 0 and kt % TJ == 0 and half == 0:
                    pe.wait_ge(k_loaded, 64 * (b * TJ + kt // TJ + 1))
                use = Use(b, kind, i, half, m=m)
                take(use)
                for e in range(2):
                    h = HG * g + 2 * half + e
                    mm = pe.matmul(use.tile[:, e, :], k_stack[:, h, kt * P:(kt + 1) * P], q_stack[:, h, :],
                                   start=True, stop=True)
                mm.then_inc(filled, 1)

            def denominators(n, m):
                pe.wait_ge(pairs_ready, n * PAIRS + m + 1 + 2)
                k = m % (KT // 2)
                for j in range(HG):
                    mm = pe.matmul(den_ps[DH * j:DH * (j + 1), :], ones[:, 0:DH], pairs[:, m % 2, j, :],
                                   start=(k == 0), stop=(k == KT // 2 - 1))
                mm.then_inc(den_done, 1)

            def weighted_values(n, i, probs_made):
                g, kt = divmod(i, KT)
                probs_made.wait_drained(pe)
                if kt == 0:
                    pe.wait_ge(ctx_copied, n * G + g + 1)
                for j in range(HG):
                    h = HG * g + j
                    mm = pe.matmul(ctx_ps[DH * j:DH * (j + 1), :], v_sb[:, kt, DH * h:DH * (h + 1)],
                                   probs[:, i % PR, j, :], start=(kt == 0), stop=(kt == KT - 1))
                mm.then_inc(pv_done, 1)

            def post(tag, n, where):
                use = where(tag)
                take(use)
                if tag[0] == "A":
                    pe.wait_ge(ctx_ready, G * (n + 1))
                    for j in (2 * int(tag[1]), 2 * int(tag[1]) + 1):
                        for g in range(G):
                            mm = pe.matmul(bank2(use.slot, D)[:, j % 2, :], ctxT[:, g, j * P:(j + 1) * P],
                                           wo_sb[:, g, :], start=(g == 0), stop=(g == G - 1))
                    mm.then_inc(filled, 1)
                elif tag == "B":
                    pe.wait_ge(y_ready, n + 1)
                    for k in range(KD):
                        for j in range(TJ):
                            mm = pe.transpose(use.tile[:, k, j * P:(j + 1) * P], y[:, j, k * P:(k + 1) * P], ident[:])
                    mm.then_inc(filled, 1)
                elif tag[0] == "C":
                    where("B").wait_drained(pe)
                    c = int(tag[1])
                    for k in range(KD):
                        mm = pe.matmul(use.tile[:, 0, :], w1_sb[:, k, c * P:(c + 1) * P], yT[:, k, :],
                                       start=(k == 0), stop=(k == KD - 1))
                    mm.then_inc(filled, 1)
                else:
                    half, j = divmod(int(tag[1]), TJ)
                    chunks = range(half * FC // 2, (half + 1) * FC // 2)
                    where(f"C{chunks[-1]}").wait_drained(pe)
                    for c in chunks:
                        mm = pe.matmul(use.tile[:, 0, 0:D], mlp[:, c, j * P:(j + 1) * P], w2_sb[:, c, :],
                                       start=(c == chunks[0]), stop=(c == chunks[-1]))
                    mm.then_inc(filled, 1)

            def products(n, i, probs_made):
                if i >= DEN_LAG and i % 2 == 0:
                    denominators(n, (i - DEN_LAG) // 2)
                if i >= LAG:
                    weighted_values(n, i - LAG, probs_made)

            def unit(b, q, kind, m):
                n = b * QT + q
                for i in range(STEPS):
                    scores(b, q, kind, m, i, 0)
                    for tag in at(i, *([POST_PE] if kind != "first" else []), *([MASK_PE] if kind != "final" else [])):
                        if tag[0] == "M":
                            mask_transposes(Use(b, kind, tag, m=m), n + 1, int(tag[1]))
                        else:
                            post(tag, n - 1, lambda t: Use(b, kind, t, m=m))
                    scores(b, q, kind, m, i, 1)
                    if i < TAIL and kind != "first":
                        products(n - 1, STEPS + i, Use(b, kind, STEPS + i - LAG, 1, m=m, unit_before=True))
                    else:
                        products(n, i, Use(b, kind, i - LAG, 1, m=m) if i >= LAG else None)
                if kind in ("last", "final"):
                    for i in range(STEPS, STEPS + TAIL):
                        products(n, i, Use(b, kind, i - LAG, 1))

            def start():
                for tag in START_PE:
                    if tag[0] == "M":
                        mask_transposes(Use(0, "start", tag), 0, int(tag[1]))
                    else:
                        chunk(tag, 0, lambda t: Use(0, "start", t))
                Use(0, "start", f"V{TJ - 1}").wait_drained(pe)

            def between(b):
                for tag in TURN_PE:
                    if tag in POST_TAGS:
                        post(tag, b * QT + QT - 1, lambda t: Use(b, "turn", t))
                    else:
                        chunk(tag, b + 1, lambda t: Use(b, "turn", t))
                Use(b, "turn", f"V{TJ - 1}").wait_drained(pe)

            def last_post(b):
                for tag in POST_TAGS:
                    post(tag, b * QT + QT - 1, lambda t: Use(b, "post", t))

            program(pe, start, unit, between, last_post)

            def general_unit(b, q, u, n):
                t = u * GENERAL
                turned = ring[0][:].rearrange("p a t -> p (a t)").bitcast(BF16).rearrange("p (k t) -> p k t", t=T)
                for piece in range(TJ):
                    pe.wait_ge(turn, t + piece * PIECE + 33 + 1)
                    for k in range(TJ):
                        for j in range(TJ):
                            mm = pe.transpose(turned[:, k, j * P:(j + 1) * P], cols_sign[:, j, k * P:(k + 1) * P],
                                              ident16[:])
                    mm.then_inc(turn, 1)
                with pe.Fori(0, H) as h:
                    th = t + MASKED + h * HEAD
                    with pe.Fori(0, KT) as k:
                        pe.wait_ge(turn, th + 51 + k * PASS1 + 1 + 1)
                        pe.matmul(ctx_ps[:], gen_k_tile, gen_q, start=True, stop=True).then_inc(turn, 1)
                    with pe.Fori(0, KT) as k:
                        tk = th + SUMS + k * PASS2
                        pe.wait_ge(turn, tk + 2 + 1)
                        pe.matmul(ctx_ps[:], gen_k_tile, gen_q, start=True, stop=True).then_inc(turn, 1)
                        pe.wait_ge(turn, tk + 7 + 1)
                        pe.matmul(den_ps[0:DH, :], gen_v_tile, gen_s, start=True, stop=True)
                        pe.matmul(ring[0][0:DH, 0, :], ones[:, 0:DH], gen_s, start=True, stop=True).then_inc(turn, 1)
                for tag in POST_TAGS:
                    post(tag, n, lambda t: GeneralUse(u, t))

            general(pe, general_unit)

        @block.scalar
        def _(act):
            act.wait_ge(weights_loaded, 16 * N_WEIGHTS)
            act.mul(qk_bias[:], qk_bias[:], QK_SCALE).then_inc(bias_scaled, 1)
            act.wait_ge(bias_scaled, 1)

            def sign(n, piece, before):
                act.wait_ge(cols_loaded, 16 * (n * TJ + piece + 1))
                if piece:
                    before.wait_filled(act)
                else:
                    act.wait_ge(mask_ready, n + 1)
                act.activation(cols_sign[:], adj_cols[:], ACT.Sign).then_inc(cols_signed, 1)

            def chunk(tag, b, use):
                use.wait_filled(act)
                c = int(tag[-1])
                n = b * 2 * TJ + 2 * c
                if tag[0] == "T":
                    act.activation(hT, use.tile[:], ACT.Copy).then_inc(drained[use.slot], 1)
                elif tag[0] in "QK":
                    o = "QK".index(tag[0])
                    act.wait_ge(low_ready, (n + o - 1 if c else n) + 1)
                    act.wait_ge(qk_stored[o], 48 * (b * TJ + c) + 1)
                    act.wait_ge(square_ready, (n + o - 1 if c else n) + 1)
                    for g in range(G):
                        a = act.activation(qk32[o][:, g, :], use.tile[:, g, :], ACT.Identity,
                                           bias=qk_bias[:, o * G + g:o * G + g + 1], scale=QK_SCALE)
                    a.then_inc(drained[use.slot], 1)
                else:
                    if c == 0:
                        act.wait_ge(v_stored, 16 * b + 1)
                    act.activation(v_sb[:, c * TJ:(c + 1) * TJ, :], bank2(use.slot, D), ACT.Copy) \
                        .then_inc(drained[use.slot], 1)

            def post(tag, use, n):
                use.wait_filled(act)
                if tag == "B":
                    act.wait_ge(out_made, n + 1)
                    act.activation(yT[:], use.tile[:], ACT.Copy) \
                        .then_inc(drained[use.slot], 1)
                else:
                    c = int(tag[1])
                    act.activation(mlp[:, c, :], use.tile[:, 0, :], ACT.Relu, bias=mlp_bias[:, c:c + 1]) \
                        .then_inc(drained[use.slot], 1)

            def copy_sums(n, g):
                act.wait_ge(pv_done, n * STEPS + (g + 1) * KT + PR)
                act.wait_ge(den_done, n * PAIRS + (g + 1) * (KT // 2) + 1)
                act.activation(ctxT[:, g, :], ctx_ps[:], ACT.Copy)
                act.activation(rden[:], den_ps[:], ACT.Copy).then_inc(ctx_copied, 1)

            def unit(b, q, kind, m):
                n = b * QT + q
                for i in range(STEPS):
                    for half in range(2):
                        use = Use(b, kind, i, half, m=m)
                        use.wait_filled(act)
                        act.activation(use.tile[:], use.tile[:], ACT.Exp, scale=EXP_SCALE).then_inc(exp_done, 1)
                        if half == 0:
                            for tag in at(i, *([POST_ACT] if kind != "first" else []),
                                          *([MASK_ACT] if kind != "final" else [])):
                                if tag[0] == "S":
                                    piece = int(tag[1])
                                    sign(n + 1, piece, Use(b, kind, f"M{piece - 1}", m=m) if piece else None)
                                else:
                                    post(tag, Use(b, kind, tag, m=m), n - 1)
                    if i == KT + TAIL - 1:
                        copy_sums(n, 0)
                    elif i == TAIL - 1 and kind != "first":
                        copy_sums(n - 1, 1)
                if kind in ("last", "final"):
                    copy_sums(n, 1)

            def start():
                for tag in START_ACT:
                    if tag[0] == "S":
                        piece = int(tag[1])
                        sign(0, piece, Use(0, "start", f"M{piece - 1}") if piece else None)
                    else:
                        chunk(tag, 0, Use(0, "start", tag))

            def between(b):
                for tag in TURN_ACT:
                    use = Use(b, "turn", tag)
                    if tag in POST_TAGS:
                        post(tag, use, b * QT + QT - 1)
                    else:
                        chunk(tag, b + 1, use)

            def last_post(b):
                for tag in POST_ACT:
                    post(tag, Use(b, "post", tag), b * QT + QT - 1)

            program(act, start, unit, between, last_post)

            def general_unit(b, q, u, n):
                t = u * GENERAL
                for piece in range(TJ):
                    act.wait_ge(turn, t + piece * PIECE + 32 + 1)
                    act.activation(cols_sign[:], adj_cols[:], ACT.Sign).then_inc(turn, 1)
                with act.Fori(0, H) as h:
                    with act.Fori(0, KT) as k:
                        act.wait_ge(turn, t + MASKED + h * HEAD + SUMS + k * PASS2 + 5 + 1)
                        act.activation(gen_s, gen_s, ACT.Exp, scale=EXP_SCALE).then_inc(turn, 1)
                for tag in POST_ACT:
                    post(tag, GeneralUse(u, tag), n)

            general(act, general_unit)

        @block.vector
        def _(dve):
            dve.memset(ones[:], 1.0).then_inc(consts_made, 1)
            dve.memset(minus_half[:], -0.5).then_inc(half_made, 1)
            dve.memset(head_ones[:], 0.0).then_inc(consts_made, 1)
            dve.wait_ge(consts_made, 3)
            for j in range(HG):
                dve.memset(head_ones[DH * j:DH * (j + 1), DH * j:DH * (j + 1)], 1.0).then_inc(consts_made, 1)
            dve.wait_ge(weights_loaded, 16 * N_WEIGHTS)
            for k in range(KD):
                dve.tensor_scalar(yT[:, k, 0:P], ones[:], v_bias[:, k:k + 1], None, ALU.mult).then_inc(bv_spread, 1)
            dve.wait_ge(setup_full, 1)
            dve.tensor_tensor(rows[:, 5, :], rows[:, 5, :], ctx_ps[:, 0:D], ALU.add).then_inc(bo_made, 1)

            def mean_and_variance(stats_made, count, aggregated, veps_made, before,
                                  stats=stats, mean_var=mean_var, var_eps=var_eps):
                wait_apart(dve, stats_made, count)
                for j in range(TJ):
                    a = dve.bn_aggr(mean_var[:, j, :], stats[:, j, :])
                a.then_inc(aggregated, 1)
                dve.wait_ge(aggregated, before + 1)
                dve.tensor_scalar(var_eps[:], mean_var[:, :, 1], EPS, None, ALU.add).then_inc(veps_made, 1)

            def normalise(t, made, mean_var=mean_var, rstd=rstd):
                for j in range(TJ):
                    a = dve.tensor_scalar(t[:, j, :], t[:, j, :], mean_var[:, j, 0:1], rstd[:, j:j + 1],
                                          ALU.subtract, ALU.mult)
                a.then_inc(made, 1)

            def mask_from(use, n, buf, piece):
                k = n * TJ + piece
                use.wait_filled(dve)
                dve.wait_ge(rows_loaded, 16 * (k + 1))
                turned = use.tile[:].rearrange("p a t -> p (a t)").bitcast(BF16)
                rows_flat = adj_rows[:].rearrange("p j t -> p (j t)")
                dst = mask[:, bass.ds(buf * KT + piece * TJ, TJ), :].rearrange("p k t -> p (k t)")
                dve.scalar_tensor_tensor(out=dst, in0=rows_flat, scalar=0.0, in1=turned, op0=ALU.is_gt, op1=ALU.max) \
                        .then_inc(drained[use.slot], 1)

            def mask_diagonal(q, buf, last_piece):
                last_piece.wait_drained(dve)
                for j in range(TJ):
                    tile = mask[:, bass.ds(buf * KT + q * TJ + j, 1), j * P:(j + 1) * P].rearrange("p a t -> p (a t)")
                    a = dve.tensor_tensor(tile, tile, ident16[:], ALU.max)
                a.then_inc(mask_ready, 1)

            def chunk(tag, b, where):
                c = int(tag[-1])
                n = b * TJ + c
                if tag[:-1] == "stat":
                    wait_apart(dve, x_loaded[c % 2], 16 * (b * 2 + c // 2 + 1))
                    for j in range(TJ):
                        a = dve.bn_stats(chunk_stats[:, j, :], h_buf(b, c)[:, j, :])
                    a.then_inc(prep_stats, 1)
                    mean_and_variance(prep_stats, n + 1, prep_meanvar, prep_veps, n,
                                      chunk_stats, chunk_mean_var, chunk_var_eps)
                elif tag[:-1] == "norm":
                    dve.wait_ge(prep_rstd, n + 1)
                    normalise(h_buf(b, c), prep_normed, chunk_mean_var, chunk_rstd)
                    dve.wait_ge(prep_normed, n + 1)
                    dve.tensor_scalar(h_buf(b, c), h_buf(b, c), 0.0, None, ALU.max).then_inc(h_ready, 1)
                elif tag[0] == "H":
                    o = "QK".index(tag[1])
                    where(f"{tag[1]}{c}").wait_drained(dve)
                    dve.wait_ge(qk_stored[o], 48 * n + 1)
                    dve.tensor_copy(high[o], qk32[o]).then_inc(high_ready, 1)
                    dve.wait_ge(high_ready, 2 * n + o + 1)
                    dve.tensor_tensor(low[o], qk32[o], high[o], ALU.subtract).then_inc(low_ready, 1)
                else:
                    o = "QK".index(tag[1])
                    use = where(tag)
                    use.wait_filled(dve)
                    dve.tensor_reduce((norms_q, norms_k)[o][:, bass.ds(b, 1), c * G:(c + 1) * G]
                                      .rearrange("p a g -> p (a g)"), use.tile[:], AX.X, ALU.max) \
                        .then_inc(drained[use.slot], 1)

            def masked(b, q, kind, m, i, half):
                kt = i % KT
                n = b * QT + q
                if half == 0:
                    if i == 0:
                        dve.wait_ge(mask_ready, n + 1 + 1)
                    if i == 0 and kind == "first":
                        for o in range(2):
                            dve.wait_ge(h_stored[o], 16 * 2 * (b + 1))
                            dve.wait_ge(qk_stored[o], 48 * TJ * (b + 1) + 1)
                    dve.wait_ge(pv_done, n * STEPS + i + 1)
                    dve.wait_ge(pairs_ready, n * PAIRS + i // 2 + 1)
                buf = {"first": 0, "middle": 1 - m, "last": 1, "final": 1}[kind]
                use = Use(b, kind, i, half, m=m)
                if i + half:
                    dve.wait_ge(exp_done, n * 2 * STEPS + 2 * i + half + 1)
                else:
                    wait_apart(dve, exp_done, n * 2 * STEPS + 1)
                keep = mask[:, bass.ds(buf * KT + kt, 1), :]
                dve.tensor_tensor(probs[:, i % PR, 2 * half:2 * half + 2, :], use.tile[:],
                                  keep.to_broadcast([P, 2, T]), ALU.mult).then_inc(drained[use.slot], 1)

            def divide_sums(n, g, part):
                if part == 0:
                    dve.wait_ge(ctx_copied, n * G + g + 1 + 1)
                r = rden[:, part * P:(part + 1) * P]
                dve.reciprocal(r, r).then_inc(rden_ready, 1)
                if part == T // P - 1:
                    dve.wait_ge(rden_ready, (n * G + g + 1) * (T // P))
                    dve.tensor_tensor(ctxT[:, g, :], ctxT[:, g, :], rden[:], ALU.mult).then_inc(ctx_ready, 1)

            def post(tag, where, n):
                use = where(tag) if tag in RING_TAGS else None
                if tag[0] == "A":
                    use.wait_filled(dve)
                    if tag == "A0":
                        dve.wait_ge(y_loaded, 16 * (n + 1))
                    j = 2 * int(tag[1])
                    dve.tensor_tensor(y[:, j:j + 2, :], bank2(use.slot, D)[:, 0:2, :], y[:, j:j + 2, :], ALU.add) \
                        .then_inc(drained[use.slot], 1)
                    use.wait_drained(dve)
                    for j in (j, j + 1):
                        a = dve.bn_stats(stats[:, j, :], y[:, j, :])
                    a.then_inc(y_stats, 1)
                    if tag == "A1":
                        mean_and_variance(y_stats, 2 * (n + 1), y_meanvar, y_veps, n)
                elif tag == "N1":
                    dve.wait_ge(y_rstd, n + 1)
                    normalise(y, y_normed)
                elif tag == "B1":
                    dve.wait_ge(y_scaled, n + 1)
                    dve.tensor_tensor(y[:], y[:], row(1), ALU.add).then_inc(y_ready, 1)
                elif tag[0] == "D":
                    half, j = divmod(int(tag[1]), TJ)
                    use.wait_filled(dve)
                    if half == 0 and j == 0:
                        dve.wait_ge(z_ready, n + 1)
                    elif half:
                        where(f"D{j}").wait_drained(dve)
                    a = dve.tensor_tensor(z[:, j, :], use.tile[:, 0, 0:D], z[:, j, :], ALU.add)
                    a.then_inc(drained[use.slot], 1)
                    if half:
                        use.wait_drained(dve)
                        dve.bn_stats(stats[:, j, :], z[:, j, :]).then_inc(z_stats, 1)
                        if j == TJ - 1:
                            mean_and_variance(z_stats, (n + 1) * TJ, z_meanvar, z_veps, n)
                elif tag == "N2":
                    dve.wait_ge(z_rstd, n + 1)
                    normalise(z, z_normed)
                elif tag == "OUT":
                    dve.wait_ge(z_normed, n + 1)
                    dve.tensor_tensor(z[:], z[:], row(2), ALU.mult).then_inc(z_scaled, 1)
                    dve.wait_ge(z_scaled, 2 * n + 1)
                    dve.tensor_tensor(z[:], z[:], row(3), ALU.add).then_inc(z_scaled, 1)
                    dve.wait_ge(z_scaled, 2 * n + 2)
                    dve.wait_ge(xres_loaded, 16 * (n + 1))
                    dve.tensor_tensor(z[:], z[:], x_res, ALU.add).then_inc(out_made, 1)

            def unit(b, q, kind, m):
                n = b * QT + q
                nxt = {"first": 1, "middle": m, "last": 0}.get(kind)
                for i in range(STEPS):
                    masked(b, q, kind, m, i, 0)
                    for tag in at(i, *([POST_DVE] if kind != "first" else []),
                                  *([MASK_DVE] if kind != "final" else []),
                                  *([NEXT_DVE] if kind == "last" else [])):
                        if tag[0] == "M":
                            mask_from(Use(b, kind, tag, m=m), n + 1, nxt, int(tag[1]))
                        elif tag == "EYE":
                            mask_diagonal(0 if kind == "last" else q + 1, nxt, Use(b, kind, "M3", m=m))
                        elif tag in NEXT_DVE:
                            chunk(tag, b + 1, None)
                        else:
                            post(tag, lambda t: Use(b, kind, t, m=m), n - 1)
                    if 0 <= i - KT - TAIL < T // P:
                        divide_sums(n, 0, i - KT - TAIL)
                    elif 0 <= i - TAIL < T // P and kind != "first":
                        divide_sums(n - 1, 1, i - TAIL)
                    masked(b, q, kind, m, i, 1)
                if kind in ("last", "final"):
                    for part in range(T // P):
                        divide_sums(n, 1, part)

            def start():
                for tag in START_DVE:
                    if tag[0] == "M":
                        mask_from(Use(0, "start", tag), 0, 0, int(tag[1]))
                    else:
                        chunk(tag, 0, lambda t: Use(0, "start", t))
                mask_diagonal(0, 0, Use(0, "start", f"M{TJ - 1}"))

            def between(b):
                for tag in TURN_DVE:
                    if tag in POST_DVE:
                        post(tag, lambda t: Use(b, "turn", t), b * QT + QT - 1)
                    else:
                        chunk(tag, b + 1, lambda t: Use(b, "turn", t))

            def last_post(b):
                for tag in POST_DVE:
                    post(tag, lambda t: Use(b, "post", t), b * QT + QT - 1)

            program(dve, start, unit, between, last_post)

            (Use(B - 2, "turn", f"NK{TJ - 1}") if B > 1 else Use(0, "start", f"NK{TJ - 1}")).wait_drained(dve)
            dve.tensor_tensor(products[:], norms_q[:], norms_k[:], ALU.mult).then_inc(products_made, 1)
            dve.wait_ge(products_made, 1)
            dve.tensor_scalar(products[:], products[:], SAFE_PRODUCT, None, ALU.is_le).then_inc(products_made, 1)
            dve.tensor_scalar(norms_q[:], norms_q[:], SAFE_NORM, None, ALU.is_le).then_inc(products_made, 1)
            dve.tensor_scalar(norms_k[:], norms_k[:], SAFE_NORM, None, ALU.is_le).then_inc(products_made, 1)
            dve.wait_ge(products_made, 4)
            for i, t in enumerate((products, norms_q, norms_k)):
                dve.tensor_reduce(unsafe[:, i:i + 1], t[:].rearrange("p b n -> p (b n)"), AX.X, ALU.min) \
                    .then_inc(products_made, 1)
            dve.wait_ge(products_made, 7)
            dve.tensor_reduce(unsafe[:, 3:4], unsafe[:, 0:3], AX.X, ALU.min).then_inc(products_made, 1)
            dve.wait_ge(products_made, 8)
            dve.tensor_scalar(unsafe[:, 0:1], unsafe[:, 3:4], -1.0, 1.0, ALU.mult, ALU.add).then_inc(products_made, 1)
            dve.wait_ge(flag_spread, 1)
            dve.tensor_copy(unsafe_int[:], unsafe[:, 1:2]).then_inc(flag_made, 1)

            def general_unit(b, q, u, n):
                t = u * GENERAL
                turned = ring[0][:].rearrange("p a t -> p (a t)").bitcast(BF16)
                for piece in range(TJ):
                    dve.wait_ge(turn, t + piece * PIECE + 34 + 1)
                    dve.scalar_tensor_tensor(
                        out=mask[:, piece * TJ:(piece + 1) * TJ, :].rearrange("p k t -> p (k t)"),
                        in0=adj_rows[:].rearrange("p j t -> p (j t)"), scalar=0.0, in1=turned,
                        op0=ALU.is_gt, op1=ALU.max).then_inc(turn, 1)
                dve.wait_ge(turn, t + MASKED - 1 + 1)
                for j in range(TJ):
                    tile = mask[:, bass.ds(q * TJ + j, 1), j * P:(j + 1) * P].rearrange("p a t -> p (a t)")
                    a = dve.tensor_tensor(tile, tile, ident16[:], ALU.max)
                a.then_inc(turn, 1)
                with dve.Fori(0, H) as h:
                    th = t + MASKED + h * HEAD
                    dve.wait_ge(turn, th + 48 + 1)
                    dve.memset(gen_max, LOWEST).then_inc(turn, 1)
                    dve.memset(gen_ctx, 0.0).then_inc(turn, 1)
                    dve.memset(gen_den, 0.0).then_inc(turn, 1)
                    with dve.Fori(0, KT) as k:
                        tk = th + 51 + k * PASS1
                        keep = mask[:, bass.ds(k, 1), :].rearrange("p a t -> p (a t)")
                        dve.wait_ge(turn, tk + 1)
                        dve.tensor_copy(gen_k_tile, gen_k[:, bass.ds(k * P, P)]).then_inc(turn, 1)
                        dve.wait_ge(turn, tk + 2 + 1)
                        dve.tensor_scalar(gen_bias, keep, -1.0, -LOWEST, ALU.add, ALU.mult).then_inc(turn, 1)
                        dve.wait_ge(turn, tk + 3 + 1)
                        dve.tensor_tensor(gen_s, ctx_ps[:], gen_bias, ALU.add).then_inc(turn, 1)
                        dve.wait_ge(turn, tk + 4 + 1)
                        dve.tensor_tensor(gen_max, gen_max, gen_s, ALU.max).then_inc(turn, 1)
                    with dve.Fori(0, KT) as k:
                        tk = th + SUMS + k * PASS2
                        keep = mask[:, bass.ds(k, 1), :].rearrange("p a t -> p (a t)")
                        dve.wait_ge(turn, tk + 1)
                        dve.tensor_copy(gen_k_tile, gen_k[:, bass.ds(k * P, P)]).then_inc(turn, 1)
                        dve.tensor_copy(gen_v_tile, gen_v[:, bass.ds(k, 1), :].rearrange("p a d -> p (a d)")) \
                            .then_inc(turn, 1)
                        dve.wait_ge(turn, tk + 3 + 1)
                        dve.tensor_tensor(gen_s, ctx_ps[:], gen_bias, ALU.subtract).then_inc(turn, 1)
                        dve.wait_ge(turn, tk + 4 + 1)
                        dve.tensor_scalar(gen_s, gen_s, 0.0, None, ALU.min).then_inc(turn, 1)
                        dve.wait_ge(turn, tk + 6 + 1)
                        dve.tensor_tensor(gen_s, gen_s, keep, ALU.mult).then_inc(turn, 1)
                        dve.wait_ge(turn, tk + 8 + 1)
                        dve.tensor_tensor(gen_ctx[0:DH, :], den_ps[0:DH, :], gen_ctx[0:DH, :], ALU.add) \
                            .then_inc(turn, 1)
                        dve.tensor_tensor(gen_den[0:DH, :], ring[0][0:DH, 0, :], gen_den[0:DH, :], ALU.add) \
                            .then_inc(turn, 1)
                    dve.wait_ge(turn, th + HEAD - 18 + 1)
                    dve.reciprocal(gen_den[0:DH, :], gen_den[0:DH, :]).then_inc(turn, 1)
                    dve.wait_ge(turn, th + HEAD - 17 + 1)
                    dve.tensor_tensor(gen_out[0:DH, :], gen_ctx[0:DH, :], gen_den[0:DH, :], ALU.mult) \
                        .then_inc(turn, 1)
                dve.wait_ge(turn, t + GENERAL + 1)
                for g in range(G):
                    dve.tensor_copy(ctxT[:, g, :], gen_ctxT[:, g, :]).then_inc(ctx_ready, 1)
                for tag in POST_DVE:
                    post(tag, lambda t: GeneralUse(u, t), n)

            general(dve, general_unit)

        @block.gpsimd
        def _(gp):
            gp.memset(ident[:], 0.0).then_inc(consts_made, 1)
            gp.wait_ge(consts_made, 3)
            gp.affine_select(out=ident[:], in_=ident[:], compare_op=ALU.not_equal, fill=1.0, base=0,
                             pattern=[[-1, P]], channel_multiplier=1).then_inc(consts_made, 1)
            gp.wait_ge(consts_made, 8)
            gp.tensor_copy(ident16[:], ident[:]).then_inc(consts_made, 1)
            for semaphore in (*drained, *qk_stored, mask_ready, cols_signed, out_made, out_stored, v_stored,
                              ctx_copied, den_done, low_ready, square_ready, turn):
                gp.sem_inc(semaphore, 1)
            gp.sem_inc(pv_done, PR)
            gp.sem_inc(pairs_ready, 2)
            gp.wait_ge(half_made, 1)

            def inverse_deviation(veps_made, made, n, var_eps=var_eps, rstd=rstd):
                gp.wait_ge(veps_made, n + 1)
                gp.tensor_tensor(rstd[:], var_eps[:], minus_half[:], ALU.pow).then_inc(made, 1)

            def chunk(tag, b, where):
                c = int(tag[-1])
                n = b * TJ + c
                if tag[:-1] == "pow":
                    inverse_deviation(prep_veps, prep_rstd, n, chunk_var_eps, chunk_rstd)
                elif tag[:-1] == "res":
                    gp.wait_ge(h_ready, n + 1)
                    gp.wait_ge(filled, where(f"T{c}").count)
                    gp.wait_ge(bo_made, 1)
                    gp.tensor_tensor(h_buf(b, c), h_buf(b, c), row(5), ALU.add).then_inc(hres_made, 1)
                else:
                    o = "QK".index(tag[1])
                    where(f"{tag[1]}{c}").wait_drained(gp)
                    if c:
                        where(f"N{tag[1]}{c - 1}").wait_filled(gp)
                    gp.tensor_tensor(square[o], qk32[o], qk32[o], ALU.mult).then_inc(square_ready, 1)

            def pair(n, m, probs_made):
                probs_made.wait_drained(gp)
                gp.wait_ge(den_done, (n * PAIRS + m - 1 if m >= 2 else n * PAIRS) + 1)
                a = (2 * m) % PR
                gp.tensor_tensor(pairs[:, m % 2], probs[:, a], probs[:, a + 1], ALU.add).then_inc(pairs_ready, 1)

            def post(tag, n):
                if tag == "R1":
                    inverse_deviation(y_veps, y_rstd, n)
                elif tag == "G1":
                    gp.wait_ge(y_normed, n + 1)
                    gp.tensor_tensor(y[:], y[:], row(0), ALU.mult).then_inc(y_scaled, 1)
                elif tag == "X1":
                    gp.wait_ge(y_ready, n + 1)
                    gp.wait_ge(out_stored, 16 * n + 1)
                    gp.tensor_tensor(z[:], y[:], row(4), ALU.add).then_inc(z_ready, 1)
                else:
                    inverse_deviation(z_veps, z_rstd, n)

            def unit(b, q, kind, m):
                n = b * QT + q
                for i in range(STEPS):
                    for tag in at(i, *([POST_POOL] if kind != "first" else []),
                                  *([NEXT_POOL] if kind == "last" else [])):
                        if tag in NEXT_POOL:
                            chunk(tag, b + 1, None)
                        else:
                            post(tag, n - 1)
                    if i % 2:
                        pair(n, i // 2, Use(b, kind, i, 1, m=m))

            def start():
                for tag in START_POOL:
                    chunk(tag, 0, lambda t: Use(0, "start", t))

            def between(b):
                for tag in TURN_POOL:
                    if tag in POST_POOL:
                        post(tag, b * QT + QT - 1)
                    else:
                        chunk(tag, b + 1, lambda t: Use(b, "turn", t))

            def last_post(b):
                for tag in POST_POOL:
                    post(tag, b * QT + QT - 1)

            program(gp, start, unit, between, last_post)

            gp.wait_ge(products_made, 9)
            gp.partition_all_reduce(unsafe[:, 1:2], unsafe[:, 0:1], P, RMAX).then_inc(flag_spread, 1)

            def general_unit(b, q, u, n):
                with gp.Fori(0, H) as h:
                    wait_apart(gp, turn, u * GENERAL + MASKED + h * HEAD + MAXIMUM + 1)
                    gp.partition_all_reduce(gen_bias, gen_max, P, RMAX).then_inc(turn, 1)
                for tag in POST_POOL:
                    post(tag, n)

            general(gp, general_unit)


def kernel(x, adj, L0_gnn_Wqkv, L0_gnn_bqkv, L0_gnn_Wo, L0_gnn_bo, L0_gnn_ln1_g, L0_gnn_ln1_b,
           L0_gnn_W1, L0_gnn_b1, L0_gnn_W2, L0_gnn_b2, L0_gnn_ln2_g, L0_gnn_ln2_b):
    import concourse.bacc as bacc
    from concourse.bass_utils import run_bass_kernel_spmd

    def flat(a):
        return np.ascontiguousarray(a)

    arrays = {
        "x": flat(x), "adj": flat(adj),
        "wqkvT": flat(np.asarray(L0_gnn_Wqkv).T), "bqkv": flat(L0_gnn_bqkv),
        "woT": flat(np.asarray(L0_gnn_Wo).T), "bo": flat(L0_gnn_bo),
        "g1": flat(L0_gnn_ln1_g), "b1n": flat(L0_gnn_ln1_b),
        "w1T": flat(np.asarray(L0_gnn_W1).T), "b1": flat(L0_gnn_b1),
        "w2T": flat(np.asarray(L0_gnn_W2).T), "b2": flat(L0_gnn_b2),
        "g2": flat(L0_gnn_ln2_g), "b2n": flat(L0_gnn_ln2_b),
    }
    nc = bacc.Bacc("TRN2", target_bir_lowering=False, num_devices=1)
    args = [nc.dram_tensor(f"in_{k}", a.shape, mybir.dt.from_np(a.dtype), kind="ExternalInput").ap()
            for k, a in arrays.items()]
    out = nc.dram_tensor("out", x.shape, F32, kind="ExternalOutput").ap()
    gnn_layer(nc, *args, out)
    r = run_bass_kernel_spmd(nc, [{f"in_{k}": a for k, a in arrays.items()}], core_ids=[0])
    return r.results[0]["out"]
```
